# Optimizing a Trainium2 kernel written in Bass

```python
import numpy as np
import jax
import jax.numpy as jnp

def _softmax(x, axis=-1):
    return jax.nn.softmax(x, axis=axis)

def _gelu(x):
    return jax.nn.gelu(x, approximate=True)

def _silu(x):
    return jax.nn.silu(x)

def _sigmoid(x):
    return jax.nn.sigmoid(x)

def _layernorm(x, axis=-1, eps=1e-05):
    m = jnp.mean(x, axis=axis, keepdims=True)
    v = jnp.var(x, axis=axis, keepdims=True)
    return (x - m) / jnp.sqrt(v + eps)

def _scatter_add(tgt, idx, src, axis=0):
    return tgt.at[idx].add(src)

def _segment_sum(src, seg, n):
    return jax.ops.segment_sum(src, seg, n)
kernel_name = 'mk_adj_preln_d2_adj_r2_a79ab7'

def setup_inputs(seed: int=0):
    np.random.seed(seed)
    _w = jnp.asarray

    def _rec_inputs():
        import jax
        import jax.numpy as jnp
        _gk = jax.random.key(seed)
        x = 7.22e-05 + 1 * jax.random.normal(jax.random.fold_in(_gk, 1), (16, 512, 128), jnp.float32)
        _w = (1.0 + jnp.arange(512, dtype=jnp.float32)) ** (-0.5)
        _w = _w / _w.mean()
        _pij = jnp.clip(0.00390625 * _w[:, None] * _w[None, :], 0.0, 1.0)
        _a = jax.random.uniform(jax.random.fold_in(_gk, 2), (512, 512)) < _pij
        _a = jnp.logical_or(_a, jnp.swapaxes(_a, -1, -2))
        _a = jnp.logical_or(_a, jnp.eye(512, dtype=bool))
        _af = _a.astype(jnp.float32)
        _af = _af * jax.random.uniform(jax.random.fold_in(_gk, 3), (512, 512), jnp.float32, 0.05, 0.000976562)
        adj = _af
        return (x, adj)
    x, adj = _rec_inputs()

    def _L0_gnn_setup():
        import jax, jax.numpy as jnp
        import numpy as np
        N_STEPS = 8
        SPATIAL_SCALE = 1.0
        key = jax.random.key(seed)
        ks = jax.random.split(key, 6)
        B, N, D = (32, 512, 128)
        x = jax.random.normal(ks[0], (B, N, D), dtype=jnp.float32)
        adj_mx = jax.random.uniform(ks[1], (N, N), dtype=jnp.float32) / N
        alpha_train = jnp.ones((N,), dtype=jnp.float32)
        w = jnp.eye(D, dtype=jnp.float32) + 0.01 * jax.random.normal(ks[2], (D, D), dtype=jnp.float32)
        d = jax.random.uniform(ks[3], (D,), dtype=jnp.float32)
        fc_in_w = jax.random.normal(ks[4], (D, D), dtype=jnp.float32) * (1.0 / np.sqrt(D))
        fc_in_b = jnp.zeros((D,), dtype=jnp.float32)
        return {'x': x, 'adj_mx': adj_mx, 'alpha_train': alpha_train, 'w': w, 'd': d, 'fc_in_w': fc_in_w, 'fc_in_b': fc_in_b, 'vt': 0}
    _L0_gnn_all = _L0_gnn_setup()
    _L0_gnn_in = {k: v for k, v in _L0_gnn_all.items() if k in ('alpha_train', 'w', 'd', 'fc_in_w', 'fc_in_b')}
    del _L0_gnn_all

    def _L1_gnn_setup():
        import jax, jax.numpy as jnp
        import numpy as np
        B, N, IN_DIM, OUT_DIM, H = (2, 2048, 128, 128, 4)
        HEAD_DIM = OUT_DIM // H
        EDGE_P = 0.01
        key = jax.random.key(seed)
        k1, k2, k3 = jax.random.split(key, 3)
        h = jax.random.normal(k1, (B, N, IN_DIM), dtype=jnp.float32)
        W = jax.random.normal(k2, (IN_DIM, 3 * OUT_DIM), dtype=jnp.float32) / np.sqrt(IN_DIM)
        adj = (jax.random.uniform(k3, (N, N)) < EDGE_P).astype(jnp.float32)
        adj = jnp.maximum(adj, jnp.eye(N, dtype=jnp.float32))
        return {'h': h, 'W': W, 'adj': adj}
    _L1_gnn_all = _L1_gnn_setup()
    _L1_gnn_in = {k: v for k, v in _L1_gnn_all.items() if k in ('W',)}
    del _L1_gnn_all
    return {'x': x, 'adj': adj, 'L0_gnn_alpha_train': _L0_gnn_in['alpha_train'], 'L0_gnn_w': _L0_gnn_in['w'], 'L0_gnn_d': _L0_gnn_in['d'], 'L0_gnn_fc_in_w': _L0_gnn_in['fc_in_w'], 'L0_gnn_fc_in_b': _L0_gnn_in['fc_in_b'], 'L1_gnn_W': _L1_gnn_in['W']}

def reference(x, adj, L0_gnn_alpha_train, L0_gnn_w, L0_gnn_d, L0_gnn_fc_in_w, L0_gnn_fc_in_b, L1_gnn_W):
    import jax
    import jax.numpy as jnp

    def _L0_gnn_ref(x, adj_mx, alpha_train, w, d, fc_in_w, fc_in_b, vt):
        import jax, jax.numpy as jnp
        import numpy as np
        N_STEPS = 8
        SPATIAL_SCALE = 1.0
        x0 = jax.lax.stop_gradient(x)
        h = jnp.einsum('bnd,ed->bne', x, fc_in_w) + fc_in_b
        alph = jax.nn.sigmoid(alpha_train)[:, None]
        d_clamped = jnp.clip(d, 0.0, 1.0)
        w_eff = w * d_clamped @ w.T
        dt = jnp.float32(SPATIAL_SCALE / N_STEPS)

        def euler_step(h, _):
            ax = jnp.einsum('nm,bmd->bnd', adj_mx, h)
            f = alph * 0.5 * (ax - h) + h @ w_eff - h + x0
            return (h + dt * f, None)
        h, _ = jax.lax.scan(euler_step, h, None, length=N_STEPS)
        return h

    def _L1_gnn_ref(h, W, adj):
        import jax, jax.numpy as jnp
        import numpy as np
        B, N, IN_DIM, OUT_DIM, H = (2, 2048, 128, 128, 4)
        HEAD_DIM = OUT_DIM // H
        EDGE_P = 0.01
        Bn, Nn, _ = h.shape
        qkv = h @ W
        qkv = qkv.reshape(Bn, Nn, 3, H, HEAD_DIM).transpose(2, 0, 3, 1, 4)
        q, k, v = (qkv[0], qkv[1], qkv[2])
        mask = jnp.where(adj == 0, -jnp.inf, 0.0)
        scores = jnp.einsum('bhid,bhjd->bhij', q, k) / np.sqrt(HEAD_DIM) + mask
        attn = jax.nn.softmax(scores, axis=-1)
        out = jnp.einsum('bhij,bhjd->bhid', attn, v)
        return out.transpose(0, 2, 1, 3).reshape(Bn, Nn, OUT_DIM)
    h = jnp.maximum(_layernorm(x, axis=-1), 0.0)
    x = x + _L0_gnn_ref(h, adj, L0_gnn_alpha_train, L0_gnn_w, L0_gnn_d, L0_gnn_fc_in_w, L0_gnn_fc_in_b, 0)
    h = jnp.maximum(_layernorm(x, axis=-1), 0.0)
    x = x + _L1_gnn_ref(h, L1_gnn_W, adj)
    return x

_drawn_inputs = setup_inputs


def setup_inputs(seed=0):
    import zlib

    import numpy as np

    out = dict(_drawn_inputs(seed))
    spreads = {'L0_gnn_alpha_train': (1.0, 0.2), 'L0_gnn_fc_in_b': (0.0, 0.1)}
    factors = {}
    for name, (base, spread) in spreads.items():
        noise = np.random.default_rng([zlib.crc32(name.encode()), seed]).standard_normal(out[name].shape)
        drawn = base * np.exp(spread * noise) if base else spread * noise
        out[name] = jnp.asarray(drawn.astype(out[name].dtype))
    for name, factor in factors.items():
        out[name] = (out[name] * factor).astype(out[name].dtype)
    return out
```

```python
from contextlib import ExitStack

import concourse.bass as bass
from concourse import mybir

F32 = mybir.dt.float32
F32R = mybir.dt.float32r
ALU = mybir.AluOpType
ACT = mybir.ActivationFunctionType

B, N, D = 16, 512, 128
HEADS = 4
HD = D // HEADS
T = N // 128
GB = 4
NG = B // GB
STEPS = 8
DT = 1.0 / STEPS
NC = STEPS + 1
EPS = 1e-5
NEG = -1e30
SCALE = float(HD) ** -0.5
CW = D + 1
CREDIT = 1
LOOP_BATCHES = 2


def wait(eng, sem, value):
    if isinstance(value, int) and value <= 0:
        return
    eng.wait_ge(sem, value)


def settle(eng, waits_met):
    eng.sem_inc(waits_met, 1)


def batch_of(ap, b):
    return ap[b:b + 1] if isinstance(b, int) else ap[bass.ds(b, 1)]


def split3(eng, psum, pairs, first=True, last=True):
    mm = None
    for n, ((lh, ll), (rh, rl)) in enumerate(pairs):
        eng.matmul(psum, lh, rh, start=(first and n == 0), stop=False)
        eng.matmul(psum, lh, rl, start=False, stop=False)
        mm = eng.matmul(psum, ll, rh, start=False, stop=(last and n == len(pairs) - 1))
    return mm


def setup_block(nc, ctx, adj, alpha, w, d, fcw, fcb, wqkv, keep):
    def sb(name, shape, dt=F32):
        return ctx.enter_context(nc.sbuf_tensor(name, shape, dt))

    def sem(name):
        return ctx.enter_context(nc.semaphore(name))

    a_nat = sb("a_nat", [128, T, N])
    alpha_sb = sb("alpha_sb", [128, T])
    s_col = sb("s_col", [128, T])
    e_col = sb("e_col", [128, T])
    c_col = sb("c_col", [128, T])
    w_sb = sb("w_sb", [128, D])
    d_sb = sb("d_sb", [128, 1])
    d_dt = sb("d_dt", [128, 1])
    w_qkv = sb("w_qkv", [128, 3 * D])
    p_nat = sb("p_nat", [128, T, N])
    p_h = sb("p_h", [128, T, N], F32R)
    p_l = sb("p_l", [128, T, N], F32R)
    w_t = sb("w_t", [128, D])
    w_td = sb("w_td", [128, D])
    q_sb = sb("q_sb", [128, D])
    coef = [sb(f"coef{i}", [128, NC + 1, CW]) for i in range(2)]
    pick = sb("pick", [128, 2, 3], F32R)
    s_rows = sb("s_rows", [3, N])
    c_rows = sb("c_rows", [3, 3 * D])

    ps_p = [ctx.enter_context(nc.psum_tensor(f"ps_p{i}", [128, 512], F32)) for i in range(4)]
    ps_c = ctx.enter_context(nc.psum_tensor("ps_c", [128, 3, 512], F32))
    ps_w = ctx.enter_context(nc.psum_tensor("ps_w", [128, 512], F32))

    adj_in, alpha_in, w_in, f_in, q_in = (sem(n) for n in ("adj_in", "alpha_in", "w_in", "f_in", "q_in"))
    exp_done, col_done, ident_done, coef_zero = (sem(n) for n in ("exp_done", "col_done", "ident_done", "coef_zero"))
    p_done, ph_done, pl_done = (sem(n) for n in ("p_done", "ph_done", "pl_done"))
    pow_mm, pow_h, pow_l = (sem(n) for n in ("pow_mm", "pow_h", "pow_l"))
    w_mm, w_done = sem("w_mm"), sem("w_done")
    coef_mm, coef_done, coef_ready = sem("coef_mm"), sem("coef_done"), sem("coef_ready")
    r_mm, r_h, r_l = sem("r_mm"), sem("r_h"), sem("r_l")
    row_mm, row_done, g_mm, g_done = (sem(n) for n in ("row_mm", "row_done", "g_mm", "g_done"))
    qw_h, qw_l, pick_done = sem("qw_h"), sem("qw_l"), sem("pick_done")

    ident = keep["ident"]
    block = ctx.enter_context(nc.Block())

    @block.sync
    def _(sp):
        sp.dma_start(a_nat[:, :, :], adj.rearrange("(p t) m -> p t m", t=T)).then_inc(adj_in, 16)
        sp.dma_start(w_qkv[:, :], wqkv).then_inc(q_in, 16)

    @block.gpsimd
    def _(pool):
        pool.memset(ident[:, :], 0.0).then_inc(ident_done, 1)
        pool.wait_ge(ident_done, 1)
        pool.affine_select(out=ident[:, :], in_=ident[:, :], compare_op=ALU.not_equal, fill=1.0,
                           base=0, pattern=[[-1, 128]], channel_multiplier=1).then_inc(ident_done, 1)
        for c in coef:
            pool.memset(c[:, :, :], 0.0).then_inc(coef_zero, 1)
        pool.memset(pick[:, :, :].bitcast(F32), 0.0).then_inc(pick_done, 1)
        pool.wait_ge(pick_done, 1)
        for j in range(2):
            pool.memset(pick[:, j, j + 1:j + 2].bitcast(F32), 1.0).then_inc(pick_done, 1)

    @block.scalar
    def _(act):
        act.dma_start(alpha_sb[:, :], alpha.rearrange("(p t) -> p t", t=T)).then_inc(alpha_in, 16)
        act.dma_start(w_sb[:, :], w).then_inc(w_in, 16)
        act.dma_start(d_sb[:, :], d.rearrange("(p o) -> p o", o=1)).then_inc(w_in, 16)
        act.wait_ge(coef_zero, 2)
        act.dma_start(coef[0][:, 1, 0:D], fcw).then_inc(f_in, 16)
        act.dma_start(coef[0][:, 1, D:CW], fcb.rearrange("(p o) -> p o", o=1)).then_inc(f_in, 16)
        act.wait_ge(alpha_in, 16)
        act.activation(e_col[:, :], alpha_sb[:, :], ACT.Exp, scale=-1.0).then_inc(exp_done, 1)
        act.wait_ge(q_in, 16)
        act.activation(keep["wH"][:, :], w_qkv[:, :], ACT.Copy).then_inc(qw_h, 1)
        for t in range(T):
            act.wait_ge(p_done, t + 1)
            act.activation(p_h[:, t, :], p_nat[:, t, :], ACT.Copy).then_inc(ph_done, 1)
        for k in range(3):
            for m in range(T):
                act.wait_ge(pow_mm, k * T + m + 1)
                act.activation(keep["pH"][k][:, m, :], ps_p[m][:, :], ACT.Copy).then_inc(pow_h, 1)
        for j in range(3):
            act.wait_ge(r_mm, j + 1)
            act.activation(keep["rH"][:, j, :], ps_p[j][:, 0:3 * D], ACT.Copy).then_inc(r_h, 1)
        act.wait_ge(row_mm, 1)
        act.activation(c_rows[:, :], ps_p[3][0:3, 0:3 * D], ACT.Copy).then_inc(row_done, 1)
        for t in range(T):
            act.wait_ge(g_mm, t + 1)
            act.activation(keep["g"][:, t, :], ps_p[t][:, 0:3 * D], ACT.Copy).then_inc(g_done, 1)

    @block.vector
    def _(dve):
        n_col = 0

        def col(ins):
            nonlocal n_col
            n_col += 1
            ins.then_inc(col_done, 1)
            dve.wait_ge(col_done, n_col)

        dve.wait_ge(exp_done, 1)
        col(dve.tensor_scalar(e_col[:, :], e_col[:, :], 1.0, None, ALU.add))
        col(dve.reciprocal(s_col[:, :], e_col[:, :]))
        col(dve.tensor_scalar(s_col[:, :], s_col[:, :], 0.5 * DT, None, ALU.mult))
        col(dve.tensor_scalar(c_col[:, :], s_col[:, :], -1.0, 1.0 - DT, ALU.mult, ALU.add))
        dve.wait_ge(adj_in, 16)
        dve.wait_ge(ident_done, 2)
        for t in range(T):
            dst = p_nat[:, t, :].rearrange("p (u q) -> p u q", u=T)
            src = a_nat[:, t, :].rearrange("p (q u) -> p u q", u=T)
            col(dve.tensor_scalar(dst, src, s_col[:, t:t + 1], None, ALU.mult))
            diag = p_nat[:, t, t * 128:(t + 1) * 128]
            dve.scalar_tensor_tensor(out=diag, in0=ident[:, :], scalar=c_col[:, t:t + 1], in1=diag,
                                     op0=ALU.mult, op1=ALU.add).then_inc(p_done, 1)
        dve.wait_ge(w_in, 32)
        col(dve.tensor_scalar(d_dt[:, :], d_sb[:, :], 0.0, 1.0, ALU.max, ALU.min))
        col(dve.tensor_scalar(d_dt[:, :], d_dt[:, :], DT, None, ALU.mult))
        dve.wait_ge(w_mm, 1)
        dve.tensor_copy(w_t[:, :], ps_w[:, 0:D])
        dve.tensor_scalar(w_td[:, :], ps_w[:, 0:D], d_dt[:, 0:1], None, ALU.mult).then_inc(w_done, 1)
        dve.wait_ge(w_mm, 2)
        dve.tensor_copy(q_sb[:, :], ps_w[:, 0:D]).then_inc(w_done, 1)
        dve.wait_ge(coef_zero, 2)
        for c in coef:
            dve.tensor_scalar(c[:, 0, 0:D], ident[:, :], DT, None, ALU.mult).then_inc(coef_ready, 1)
        dve.wait_ge(coef_ready, 2)
        dve.wait_ge(f_in, 32)

        def low(i):
            if i < T:
                dve.wait_ge(ph_done, i + 1)
                dve.tensor_tensor(p_l[:, i, :], p_nat[:, i, :], p_h[:, i, :].bitcast(F32),
                                  ALU.subtract).then_inc(pl_done, 1)
            else:
                k, m = divmod(i - T, T)
                dve.wait_ge(pow_h, k * T + m + 1)
                dve.tensor_tensor(keep["pL"][k][:, m, :], ps_p[m][:, :], keep["pH"][k][:, m, :].bitcast(F32),
                                  ALU.subtract).then_inc(pow_l, 1)

        def step(n):
            old, new = coef[n % 2], coef[(n + 1) % 2]
            if n:
                dve.wait_ge(coef_done, n)
            dve.tensor_copy(new[:, n + 2, :], old[:, n + 1, :])
            dve.wait_ge(coef_mm, n + 1)
            for s in range(1, n + 2, 3):
                k = min(3, n + 2 - s)
                last = dve.tensor_tensor(new[:, s:s + k, :],
                                         ps_c[:, (s - 1) // 3, 0:k * CW].rearrange("p (k c) -> p k c", c=CW),
                                         old[:, s - 1:s - 1 + k, :], ALU.add)
            last.then_inc(coef_done, 1)

        for i in range(2 * T):
            low(i)
        for n in range(STEPS):
            step(n)
            low(2 * T + n)
        dve.wait_ge(qw_h, 1)
        dve.tensor_tensor(keep["wL"][:, :], w_qkv[:, :], keep["wH"][:, :].bitcast(F32),
                          ALU.subtract).then_inc(qw_l, 1)
        for j in range(3):
            dve.wait_ge(r_h, j + 1)
            dve.tensor_tensor(keep["rL"][:, j, :], ps_p[j][:, 0:3 * D], keep["rH"][:, j, :].bitcast(F32),
                              ALU.subtract).then_inc(r_l, 1)
        dve.wait_ge(row_mm, 2)
        dve.tensor_scalar(s_rows[:, :], ps_w[0:3, :], ident[0:3, 0:1], None, ALU.add).then_inc(row_done, 1)

    @block.tensor
    def _(pe):
        pe.wait_ge(ident_done, 2)
        pe.wait_ge(w_in, 32)
        pe.transpose(ps_w[:, 0:D], w_sb[:, :], ident[:, :]).then_inc(w_mm, 1)
        pe.wait_ge(w_done, 1)
        pe.matmul(ps_w[:, 0:D], w_td[:, :], w_t[:, :], start=True, stop=True).then_inc(w_mm, 1)
        pe.wait_ge(p_done, T)
        for m in range(T):
            for t in range(T):
                tr = pe.transpose(ps_p[m][:, t * 128:(t + 1) * 128], p_nat[:, t, m * 128:(m + 1) * 128], ident[:, :])
            tr.then_inc(pow_mm, 1)
        pe.wait_ge(w_done, 2)
        pe.wait_ge(f_in, 32)
        pe.wait_ge(coef_zero, 2)
        pe.wait_ge(coef_ready, 2)

        def power(k, m):
            if m == 0:
                pe.wait_ge(pow_l, k * T)
                pe.wait_ge(ph_done, T)
                pe.wait_ge(pl_done, T)
            pairs = [((p_h[:, c, m * 128:(m + 1) * 128], p_l[:, c, m * 128:(m + 1) * 128]),
                      (keep["pH"][k - 1][:, c, :], keep["pL"][k - 1][:, c, :])) for c in range(T)]
            split3(pe, ps_p[m][:, :], pairs).then_inc(pow_mm, 1)

        for n in range(STEPS):
            if n:
                pe.wait_ge(coef_done, n)
            for s in range(1, n + 2, 3):
                k = min(3, n + 2 - s)
                mm = pe.matmul(ps_c[:, (s - 1) // 3, 0:k * CW], q_sb[:, :],
                               coef[n % 2][:, s:s + k, :].rearrange("p k c -> p (k c)"), start=True, stop=True)
            mm.then_inc(coef_mm, 1)
            power(1 + n // T, n % T)
        fin = coef[STEPS % 2]
        pe.wait_ge(coef_done, STEPS)
        pe.wait_ge(pow_l, 3 * T)
        for j in range(3):
            for i in range(3):
                tr = pe.transpose(ps_p[j][:, i * D:(i + 1) * D], fin[:, 1 + 3 * i + j, 0:D], ident[:, :])
            tr.then_inc(r_mm, 1)
        for i in range(3):
            tr = pe.transpose(ps_p[3][0:3, i * D:(i + 1) * D], fin[:, 1 + 3 * i:4 + 3 * i, D], ident[:, :])
        tr.then_inc(row_mm, 1)
        pe.wait_ge(pick_done, 3)
        for j in range(2):
            for m in range(T):
                for part in ("pH", "pL"):
                    mm = pe.matmul(ps_w[0:3, :], pick[:, j, :], keep[part][j][:, m, :],
                                   start=(j == 0 and m == 0 and part == "pH"),
                                   stop=(j == 1 and m == T - 1 and part == "pL"))
        mm.then_inc(row_mm, 1)
        pe.wait_ge(row_done, 2)
        pe.wait_ge(r_l, 3)
        for t in range(T):
            pe.matmul(ps_p[t][:, 0:3 * D], s_rows[:, t * 128:(t + 1) * 128], c_rows[:, :],
                      start=True, stop=True).then_inc(g_mm, 1)


def ode_block(nc, ctx, x, x1_dram, qk_dram, v_dram, keep):
    def sb(name, shape, dt=F32):
        return ctx.enter_context(nc.sbuf_tensor(name, shape, dt))

    def sem(name):
        return ctx.enter_context(nc.semaphore(name))

    def bank(name):
        return ctx.enter_context(nc.psum_tensor(name, [128, 512], F32))

    x_ln = [sb(f"x_ln{i}", [128, T, D]) for i in range(2)]
    x_res = sb("x_res", [128, T, D])
    u0 = sb("u0", [128, GB, T, D])
    u0_h = sb("u0_h", [128, GB, T, D], F32R)
    u0_l = sb("u0_l", [128, GB, T, D], F32R)
    ut_h = [sb(f"ut_h{i}", [128, 3, N], F32R) for i in range(2)]
    ut_l = [sb(f"ut_l{i}", [128, 3, N], F32R) for i in range(2)]
    v = sb("v", [128, T, GB, 3 * D])
    v2_h = sb("v2_h", [128, T, GB, D], F32R)
    v2_l = sb("v2_l", [128, T, GB, D], F32R)
    z_h = sb("z_h", [128, T, GB, D], F32R)
    z_l = sb("z_l", [128, T, GB, D], F32R)
    h2 = sb("h2", [128, GB, T, D])
    ht_h = [sb(f"ht_h{i}", [128, N], F32R) for i in range(2)]
    ht_l = [sb(f"ht_l{i}", [128, N], F32R) for i in range(2)]
    qk = [sb(f"qk{i}", [128, 2, N], F32R) for i in range(2)]
    vt = [sb(f"vt{i}", [128, N]) for i in range(2)]
    v_nat = sb("v_nat", [128, N])
    stat = [sb(f"stat{i}", [128, T, 6]) for i in range(2)]
    mv = [sb(f"mv{i}", [128, T, 2]) for i in range(2)]
    std = [sb(f"std{i}", [128, T]) for i in range(2)]
    eps = sb("eps", [128, 1])

    ps_u = [bank(f"ps_u{i}") for i in range(2)]
    ps_v = [bank(f"ps_v{i}") for i in range(2)]
    ps_z = [bank(f"ps_z{i}") for i in range(2)]
    ps_k = [bank(f"ps_k{i}") for i in range(2)]

    ident = keep["ident"]
    eps_done = sem("eps_done")
    waits_met = sem("waits_met")
    xl_in = [sem(f"xl_in{i}") for i in range(2)]
    xr_in = sem("xr_in")
    st_done = [sem(f"st_done{i}") for i in range(2)]
    var_done = [sem(f"var_done{i}") for i in range(2)]
    std_done = [sem(f"std_done{i}") for i in range(2)]
    rs_done = [sem(f"rs_done{i}") for i in range(2)]
    norm_done = [sem(f"norm_done{i}") for i in range(2)]
    u0_done, u0h_done, u0l_done = sem("u0_done"), sem("u0h_done"), sem("u0l_done")
    u_mm, uh_done, ul_done = sem("u_mm"), sem("uh_done"), sem("ul_done")
    v_mm, v_add, v2h_done, v2l_done, xv_done = (sem(n) for n in ("v_mm", "v_add", "v2h_done", "v2l_done", "xv_done"))
    z_mm, z_add, zh_done, zl_done = (sem(n) for n in ("z_mm", "z_add", "zh_done", "zl_done"))
    y_mm, x1_add, x1_out = sem("y_mm"), sem("x1_add"), sem("x1_out")
    h2_done = sem("h2_done")
    k_mm, kh_done, kl_done, vt_done, vn_done = (sem(n) for n in ("k_mm", "kh_done", "kl_done", "vt_done", "vn_done"))
    qk_out = [sem(f"qk_out{i}") for i in range(2)]
    v_out = sem("v_out")

    BACK = [("t", 0), ("t", 1), ("q", 0), ("k", 0), ("vt", 0), ("q", 1), ("k", 1), ("vt", 1), ("v", 0), ("v", 1)]
    NB = len(BACK)
    SPLIT = [i for i, (kind, _) in enumerate(BACK) if kind in "tqk"]
    VT = [i for i, (kind, _) in enumerate(BACK) if kind == "vt"]
    VN = [i for i, (kind, _) in enumerate(BACK) if kind == "v"]

    def freed(i, pair):
        if i in SPLIT:
            return kl_done, len(SPLIT) * pair + SPLIT.index(i) + 1
        if i in VT:
            return vt_done, len(VT) * pair + VT.index(i) + 1
        return vn_done, len(VN) * pair + VN.index(i) + 1

    def group(g, first, u, v_, ln1, ln2, back, z, y):
        def second_norm(b):
            if not first:
                ln2(g - 1, b)
        u(g, 0)
        second_norm(0)
        for b in range(1, GB):
            u(g, b)
            second_norm(b)
            v_(g, b - 1)
            ln1(g + 1, b - 1)
        v_(g, GB - 1)
        ln1(g + 1, GB - 1)
        if not first:
            back(g - 1, 0)
        for t in range(T):
            z(g, t)
        if not first:
            back(g - 1, 1)
        for t in range(T):
            y(g, t)

    def nothing(*_):
        pass

    def run(eng, u=nothing, v_=nothing, ln1=nothing, ln2=nothing, back=nothing, z=nothing, y=nothing):
        for b in range(GB):
            ln1(0, b)
        group(0, True, u, v_, ln1, ln2, back, z, y)
        with eng.Fori(1, NG - 1) as g:
            group(g, False, u, v_, ln1, ln2, back, z, y)
        group(NG - 1, False, u, v_, nothing, ln2, back, z, y)
        for b in range(GB):
            ln2(NG - 1, b)
        for pair in range(2):
            back(NG - 1, pair)

    block = ctx.enter_context(nc.Block())

    @block.sync
    def _(sp):
        def load_ln(g, b):
            wait(sp, norm_done[0], GB * g + b - 1)
            sp.dma_start(x_ln[b % 2][:, :, :], batch_of(x, GB * g + b).rearrange("o (p t) d -> p (o t) d", t=T)).then_inc(xl_in[b % 2], 16)

        def load_res(g, b):
            wait(sp, xv_done, GB * g + b)
            sp.dma_start(x_res[:, :, :], batch_of(x, GB * g + b).rearrange("o (p t) d -> p (o t) d", t=T)).then_inc(xr_in, 16)

        def second_norm(g, b):
            if b == 0:
                wait(sp, x1_add, T * (g + 1))
                for c in range(GB):
                    sp.dma_start(batch_of(x1_dram, GB * g + c).rearrange("o p t d -> p (o t) d"), v[:, :, c, 0:D]).then_inc(x1_out, 16)

        def back(g, pair):
            for i, (kind, c) in enumerate(BACK):
                b = 2 * pair + c
                if kind in ("q", "k"):
                    which = 0 if kind == "q" else 1
                    wait(sp, kl_done, len(SPLIT) * (2 * g + pair) + SPLIT.index(i) + 1)
                    dst = batch_of(qk_dram, GB * g + b)[:, :, 2 * which:2 * which + 2, :].rearrange("o p s n -> p (o s) n")
                    sp.dma_start(dst, qk[which][:, :, :].bitcast(F32)).then_inc(qk_out[which], 16)
                if kind == "v":
                    wait(sp, vn_done, 2 * (2 * g + pair) + c + 1)
                    sp.dma_start(batch_of(v_dram, GB * g + b).rearrange("o p n -> p (o n)"), v_nat[:, :]).then_inc(v_out, 16)

        for s in (*qk_out, v_out):
            sp.sem_inc(s, CREDIT)
        run(sp, v_=load_res, ln1=load_ln, ln2=second_norm, back=back)
        sp.wait_ge(x1_out, 16 * B)
        for s in (*qk_out, v_out):
            sp.wait_ge(s, CREDIT + 16 * B)

    @block.gpsimd
    def _(pool):
        pool.memset(eps[:, :], EPS).then_inc(eps_done, 1)

        def ln1(g, b):
            n = GB * g + b
            wait(pool, u0h_done, n + 1)
            wait(pool, u_mm, 3 * (n - GB) + 3)
            pool.tensor_tensor(u0_l[:, b, :, :], u0[:, b, :, :], u0_h[:, b, :, :].bitcast(F32),
                               ALU.subtract).then_inc(u0l_done, 1)

        def v_step(g, b):
            n = GB * g + b
            wait(pool, xr_in, 16 * (n + 1))
            wait(pool, v_add, T * (n + 1))
            pool.tensor_tensor(v[:, :, b, 0:D], v[:, :, b, 0:D], x_res[:, :, :], ALU.add).then_inc(xv_done, 1)
            wait(pool, v2h_done, n + 1)
            wait(pool, z_mm, T * g)
            pool.tensor_tensor(v2_l[:, :, b, :], v[:, :, b, 2 * D:3 * D], v2_h[:, :, b, :].bitcast(F32),
                               ALU.subtract).then_inc(v2l_done, 1)

        def z_step(g, t):
            wait(pool, zh_done, T * g + t + 1)
            wait(pool, y_mm, T * g)
            pool.tensor_tensor(z_l[:, t, :, :], v[:, t, :, D:2 * D], z_h[:, t, :, :].bitcast(F32),
                               ALU.subtract).then_inc(zl_done, 1)

        run(pool, v_=v_step, ln1=ln1, z=z_step)

    @block.scalar
    def _(act):
        act.wait_ge(eps_done, 1)

        def u_step(g, b):
            for k in range(3):
                n = 3 * (GB * g + b) + k
                wait(act, u_mm, n + 1)
                wait(act, v_mm, T * (GB * g + b - 1))
                act.activation(ut_h[b % 2][:, k, :], ps_u[(3 * b + k) % 2][:, :], ACT.Copy).then_inc(uh_done, 1)

        def root(i, n):
            wait(act, var_done[i], n + 1)
            act.activation(std[i][:, :], mv[i][:, :, 1], ACT.Sqrt, bias=eps[:, 0:1]).then_inc(std_done[i], 1)

        def ln1(g, b):
            n = GB * g + b
            root(0, n)
            wait(act, norm_done[0], n + 1)
            act.activation(u0[:, b, :, :], u0[:, b, :, :], ACT.Relu).then_inc(u0_done, 1)
            wait(act, u0_done, n + 1)
            wait(act, u_mm, 3 * (n - GB) + 3)
            act.activation(u0_h[:, b, :, :], u0[:, b, :, :], ACT.Copy).then_inc(u0h_done, 1)

        def ln2(g, b):
            n = GB * g + b
            root(1, n)
            wait(act, norm_done[1], n + 1)
            act.activation(h2[:, b, :, :], h2[:, b, :, :], ACT.Relu).then_inc(h2_done, 1)

        def v_step(g, b):
            n = GB * g + b
            wait(act, v_add, T * (n + 1))
            wait(act, z_mm, T * g)
            act.activation(v2_h[:, :, b, :], v[:, :, b, 2 * D:3 * D], ACT.Copy).then_inc(v2h_done, 1)

        def z_step(g, t):
            wait(act, z_add, T * g + t + 1)
            wait(act, y_mm, T * g)
            act.activation(z_h[:, t, :, :], v[:, t, :, D:2 * D], ACT.Copy).then_inc(zh_done, 1)

        def back(g, pair):
            pr = 2 * g + pair
            for i, (kind, c) in enumerate(BACK):
                wait(act, k_mm, NB * pr + i + 1)
                src = ps_k[i % 2][:, :]
                if kind == "t":
                    if pair:
                        wait(act, k_mm, NB * (pr - 1) + VT[c] + 1)
                    act.activation(ht_h[c][:, :], src, ACT.Copy).then_inc(kh_done, 1)
                elif kind in ("q", "k"):
                    which = 0 if kind == "q" else 1
                    wait(act, qk_out[which], CREDIT + 16 * (2 * pr + c))
                    act.activation(qk[which][:, 0, :], src, ACT.Copy).then_inc(kh_done, 1)
                elif kind == "vt":
                    if pair:
                        wait(act, k_mm, NB * (pr - 1) + VN[c] + 1)
                    act.activation(vt[c][:, :], src, ACT.Copy).then_inc(vt_done, 1)
                else:
                    wait(act, v_out, CREDIT + 16 * (2 * pr + c))
                    act.activation(v_nat[:, :], src, ACT.Copy).then_inc(vn_done, 1)

        run(act, u=u_step, v_=v_step, ln1=ln1, ln2=ln2, back=back, z=z_step)

    @block.vector
    def _(dve):
        def u_step(g, b):
            for k in range(3):
                n = 3 * (GB * g + b) + k
                wait(dve, uh_done, n + 1)
                wait(dve, v_mm, T * (GB * g + b - 1))
                dve.tensor_tensor(ut_l[b % 2][:, k, :], ps_u[(3 * b + k) % 2][:, :],
                                  ut_h[b % 2][:, k, :].bitcast(F32), ALU.subtract).then_inc(ul_done, 1)

        def norm(i, n, src, dst):
            for t in range(T):
                last = dve.bn_stats(stat[i][:, t, :], src(t))
            last.then_inc(st_done[i], 1)
            wait(dve, st_done[i], n + 1)
            settle(dve, waits_met)
            for t in range(T):
                last = dve.bn_aggr(mv[i][:, t, :], stat[i][:, t, :])
            last.then_inc(var_done[i], 1)
            wait(dve, std_done[i], n + 1)
            dve.reciprocal(std[i][:, :], std[i][:, :]).then_inc(rs_done[i], 1)
            wait(dve, rs_done[i], n + 1)
            wait(dve, var_done[i], n + 1)
            for t in range(T):
                last = dve.tensor_scalar(dst(t), src(t), mv[i][:, t, 0:1], std[i][:, t:t + 1],
                                         ALU.subtract, ALU.mult)
            last.then_inc(norm_done[i], 1)

        def ln1(g, b):
            n = GB * g + b
            if b < 2:
                wait(dve, xl_in[b % 2], 16 * (2 * g + 1))
            else:
                wait(dve, xl_in[b % 2], 16 * (2 * g + 2))
            wait(dve, u_mm, 3 * (n - GB) + 3)
            wait(dve, u0l_done, n - GB + 1)
            norm(0, n, lambda t: x_ln[b % 2][:, t, :], lambda t: u0[:, b, t, :])

        def ln2(g, b):
            n = GB * g + b
            wait(dve, x1_add, T * (g + 1))
            norm(1, n, lambda t: v[:, t, b, 0:D], lambda t: h2[:, b, t, :])

        def v_step(g, b):
            for t in range(T):
                n = T * (GB * g + b) + t
                wait(dve, v_mm, n + 1)
                if t == 0:
                    wait(dve, x1_out, 16 * GB * g)
                    wait(dve, norm_done[1], GB * (g - 1) + b + 1)
                    wait(dve, zl_done, T * g)
                    wait(dve, v2l_done, GB * (g - 1) + b + 1)
                dve.tensor_tensor(v[:, t, b, :], ps_v[t % 2][:, 0:3 * D], keep["g"][:, t, :],
                                  ALU.add).then_inc(v_add, 1)

        def z_step(g, t):
            wait(dve, z_mm, T * g + t + 1)
            wait(dve, v_add, T * GB * (g + 1))
            dve.tensor_tensor(v[:, t, :, D:2 * D], ps_z[t % 2][:, :].rearrange("p (b d) -> p b d", b=GB),
                              v[:, t, :, D:2 * D], ALU.add).then_inc(z_add, 1)

        def y_step(g, t):
            wait(dve, y_mm, T * g + t + 1)
            wait(dve, xv_done, GB * (g + 1))
            dve.tensor_tensor(v[:, t, :, 0:D], ps_z[t % 2][:, :].rearrange("p (b d) -> p b d", b=GB),
                              v[:, t, :, 0:D], ALU.add).then_inc(x1_add, 1)

        def back(g, pair):
            pr = 2 * g + pair
            for i, (kind, c) in enumerate(BACK):
                if i not in SPLIT:
                    continue
                wait(dve, kh_done, len(SPLIT) * pr + SPLIT.index(i) + 1)
                src = ps_k[i % 2][:, :]
                if kind == "t":
                    if pair:
                        wait(dve, k_mm, NB * (pr - 1) + VT[c] + 1)
                    dst, high = ht_l[c][:, :], ht_h[c][:, :]
                else:
                    which = 0 if kind == "q" else 1
                    wait(dve, qk_out[which], CREDIT + 16 * (2 * pr + c))
                    dst, high = qk[which][:, 1, :], qk[which][:, 0, :]
                dve.tensor_tensor(dst, src, high.bitcast(F32), ALU.subtract).then_inc(kl_done, 1)

        run(dve, u=u_step, v_=v_step, ln1=ln1, ln2=ln2, back=back, z=z_step, y=y_step)

    @block.tensor
    def _(pe):
        def u_step(g, b):
            nb = GB * g + b
            for k in range(3):
                n = 3 * nb + k
                wait(pe, ul_done, n - 1)
                ps = ps_u[(3 * b + k) % 2]
                if k == 0:
                    wait(pe, u0_done, nb + 1)
                    for t in range(T):
                        mm = pe.transpose(ps[:, t * 128:(t + 1) * 128], u0[:, b, t, :], ident[:, :])
                else:
                    wait(pe, u0l_done, nb + 1)
                    mm = split3(pe, ps[:, :], [((u0_h[:, b, m, :], u0_l[:, b, m, :]),
                                                (keep["pH"][k - 1][:, m, :], keep["pL"][k - 1][:, m, :]))
                                               for m in range(T)])
                mm.then_inc(u_mm, 1)

        def v_step(g, b):
            nb = GB * g + b
            wait(pe, ul_done, 3 * nb + 3)
            for t in range(T):
                wait(pe, v_add, T * nb + t - 1)
                rows = slice(t * 128, (t + 1) * 128)
                split3(pe, ps_v[t % 2][:, 0:3 * D], [((ut_h[b % 2][:, k, rows], ut_l[b % 2][:, k, rows]),
                                                     (keep["rH"][:, k, :], keep["rL"][:, k, :]))
                                                    for k in range(3)]).then_inc(v_mm, 1)

        def cube(g, t, src_h, src_l):
            rows = slice(t * 128, (t + 1) * 128)
            return split3(pe, ps_z[t % 2][:, :],
                          [((keep["pH"][2][:, m, rows], keep["pL"][2][:, m, rows]),
                            (src_h[:, m, :, :].rearrange("p b d -> p (b d)"),
                             src_l[:, m, :, :].rearrange("p b d -> p (b d)"))) for m in range(T)])

        def z_step(g, t):
            if t == 0:
                wait(pe, v2l_done, GB * (g + 1))
            if t < 2:
                wait(pe, x1_add, T * g - 2 + t + 1)
            else:
                wait(pe, z_add, T * g + t - 1)
            cube(g, t, v2_h, v2_l).then_inc(z_mm, 1)

        def y_step(g, t):
            if t == 0:
                wait(pe, zl_done, T * (g + 1))
            if t < 2:
                wait(pe, z_add, T * g + 2 + t + 1)
            else:
                wait(pe, x1_add, T * g + t - 1)
            cube(g, t, z_h, z_l).then_inc(y_mm, 1)

        def back(g, pair):
            pr = 2 * g + pair
            for i, (kind, c) in enumerate(BACK):
                ps = ps_k[i % 2]
                if i >= 2:
                    wait(pe, *freed(i - 2, pr))
                elif pair:
                    wait(pe, *freed(NB + i - 2, pr - 1))
                if kind == "t":
                    b = 2 * pair + c
                    wait(pe, h2_done, GB * g + b + 1)
                    for t in range(T):
                        mm = pe.transpose(ps[:, t * 128:(t + 1) * 128], h2[:, b, t, :], ident[:, :])
                elif kind == "v":
                    wait(pe, vt_done, 2 * pr + c + 1)
                    for t in range(T):
                        mm = pe.transpose(ps[:, t * 128:(t + 1) * 128], vt[c][:, t * 128:(t + 1) * 128], ident[:, :])
                else:
                    wait(pe, kl_done, len(SPLIT) * pr + c + 1)
                    at = {"q": 0, "k": D, "vt": 2 * D}[kind]
                    mm = split3(pe, ps[:, :], [((keep["wH"][:, at:at + D], keep["wL"][:, at:at + D]),
                                                (ht_h[c][:, :], ht_l[c][:, :]))])
                mm.then_inc(k_mm, 1)

        run(pe, u=u_step, v_=v_step, back=back, z=z_step, y=y_step)


def attention_block(nc, ctx, adj, x1_dram, qk_dram, v_dram, out, keep):
    def sb(name, shape, dt=F32):
        return ctx.enter_context(nc.sbuf_tensor(name, shape, dt))

    def sem(name):
        return ctx.enter_context(nc.semaphore(name))

    TILES = T * HEADS
    PAIRS = TILES // 2
    RING = 4
    LAG = 2
    ACT_PAIRS = [0, 2, 5]
    DVE_PAIRS = [p for p in range(PAIRS) if p not in ACT_PAIRS]
    PV_AT, OCOPY_AT, OT_AT, FIN_AT, STORE_AT = 4, 6, 8, 10, 14

    a_nat = sb("a_nat2", [128, T, N])
    mask = sb("mask", [128, T, N])
    q_st = [sb(f"q_st{i}", [128, HEADS, N], F32R) for i in range(2)]
    k_st = [sb(f"k_st{i}", [128, HEADS, N], F32R) for i in range(2)]
    v_sb = [sb(f"v_sb{i}", [128, T, D]) for i in range(2)]
    x1 = [sb(f"x1_{i}", [128, T * D]) for i in range(2)]
    s_ring = sb("s_ring", [128, RING, N])
    low = sb("low", [128, TILES])
    lsum = [sb(f"lsum{i}", [128, TILES]) for i in range(2)]
    p_t = [sb(f"p_t{i}", [128, HEADS, T, N]) for i in range(2)]
    o_t = sb("o_t", [128, N])
    o_n = [sb(f"o_n{i}", [128, T * D]) for i in range(2)]

    ps_s = [ctx.enter_context(nc.psum_tensor(f"ps_s{i}", [128, N], F32)) for i in range(2)]
    ps_t = [ctx.enter_context(nc.psum_tensor(f"ps_t{i}", [128, 2, N], F32)) for i in range(2)]
    ps_o = ctx.enter_context(nc.psum_tensor("ps_o", [128, N], F32))
    ps_n = ctx.enter_context(nc.psum_tensor("ps_n", [128, N], F32))

    ident = keep["ident"]
    adj_in, mask_done, waits_met = sem("adj2_in"), sem("mask_done"), sem("waits_met2")
    qk_in = [sem(f"qk_in{i}") for i in range(2)]
    v_in = [sem(f"v_in{i}") for i in range(2)]
    x_in = [sem(f"x_in{i}") for i in range(2)]
    s_mm, s_max, p_done, t_mm, t_act, t_dve = (sem(n) for n in ("s_mm", "s_max", "p_done", "t_mm", "t_act", "t_dve"))
    pv_mm, o_copy, o_mm, rl_done, o_div, o_add = (sem(n) for n in ("pv_mm", "o_copy", "o_mm", "rl_done", "o_div", "o_add"))
    o_out = [sem(f"o_out{i}") for i in range(2)]

    def run(eng, batch, tail):
        batch(0, 0)
        with eng.Fori(0, (B - 2) // LOOP_BATCHES) as turn:
            for k in range(LOOP_BATCHES):
                batch(turn * LOOP_BATCHES + (1 + k), (1 + k) % 2)
        batch(B - 1, (B - 1) % 2)
        tail(B, B % 2)

    def seen(b, par):
        return b // 2 + 1 if isinstance(b, int) else None

    def copied(p, b):
        if p in ACT_PAIRS:
            return t_act, len(ACT_PAIRS) * b + ACT_PAIRS.index(p) + 1
        return t_dve, len(DVE_PAIRS) * b + DVE_PAIRS.index(p) + 1

    def pair_after(n):
        if n % 2:
            return None
        p = (n - LAG) // 2 - 1
        return (p, 0) if p >= 0 else (p + PAIRS, 1)

    def copy_pair(eng, p, b, par):
        wait(eng, t_mm, TILES * b + 2 * p + 2)
        if p in (ACT_PAIRS[0], DVE_PAIRS[0]):
            wait(eng, pv_mm, CREDIT + b - 1)
        it, h = divmod(2 * p, HEADS)
        dst = p_t[par][:, h:h + 2, :, it * 128:(it + 1) * 128]
        src = ps_t[p % 2][:, :, :].rearrange("p h (j i) -> p h j i", j=T)
        return dst, src

    block = ctx.enter_context(nc.Block())

    @block.sync
    def _(sp):
        sp.dma_start(a_nat[:, :, :], adj.rearrange("(p t) m -> p t m", t=T)).then_inc(adj_in, 16)

        def batch(b, par):
            src = batch_of(qk_dram, b)
            wait(sp, s_mm, CREDIT + TILES * (b - 1))
            for slot in range(4):
                for st, part in ((q_st, slot // 2), (k_st, 2 + slot % 2)):
                    sp.dma_start(st[par][HD * slot:HD * (slot + 1), :, :].bitcast(F32),
                                 src[:, :, part:part + 1, :].rearrange("o (h e) s n -> e (o s h) n", e=HD)).then_inc(qk_in[par], 16)
            wait(sp, pv_mm, CREDIT + b - 1)
            sp.dma_start(v_sb[par][:, :, :].rearrange("p t d -> p (t d)"), batch_of(v_dram, b).rearrange("o p n -> p (o n)")).then_inc(v_in[par], 16)
            wait(sp, o_add, CREDIT + b - 1)
            sp.dma_start(x1[par][:, :], batch_of(x1_dram, b).rearrange("o p t d -> p (o t d)")).then_inc(x_in[par], 16)

        run(sp, batch, nothing)
        for s in o_out:
            sp.wait_ge(s, CREDIT + 16 * B // 2)

    def parity_count(b, par, each):
        if isinstance(b, int):
            return each * (b // 2 + 1)
        assert each % 2 == 0
        return b * (each // 2) + (each // 2) * (2 - par)

    @block.gpsimd
    def _(pool):
        def batch(b, par):
            if isinstance(b, int) and b == 0:
                return
            c, cp = b - 1, 1 - par
            wait(pool, o_div, CREDIT + c + 1)
            wait(pool, x_in[cp], parity_count(c, cp, 16))
            pool.tensor_tensor(o_n[cp][:, :], o_n[cp][:, :], x1[cp][:, :], ALU.add).then_inc(o_add, 1)

        pool.sem_inc(o_add, CREDIT)
        run(pool, batch, batch)

    @block.scalar
    def _(act):
        def batch(b, par, tiles=TILES):
            first = isinstance(b, int) and b == 0
            for n in range(TILES):
                if tiles:
                    wait(act, s_max, TILES * b + n + 1)
                    if n == 0:
                        wait(act, o_div, CREDIT + b - 1)
                    act.activation(s_ring[:, n % RING, :], s_ring[:, n % RING, :], ACT.Exp,
                                   bias=low[:, n:n + 1], scale=-1.0, accum_out=lsum[par][:, n:n + 1]).then_inc(p_done, 1)
                pair = pair_after(n)
                if pair and pair[0] in ACT_PAIRS and not (first and pair[1]) and (tiles or pair[1]):
                    dst, src = copy_pair(act, pair[0], b - pair[1], (par + pair[1]) % 2)
                    act.activation(dst, src, ACT.Copy).then_inc(t_act, 1)
                if n == OCOPY_AT and not first:
                    wait(act, pv_mm, CREDIT + b)
                    wait(act, o_mm, CREDIT + b - 1)
                    act.activation(o_t[:, :], ps_o[:, :], ACT.Copy).then_inc(o_copy, 1)
                if n == STORE_AT and not first:
                    wait(act, o_add, CREDIT + b)
                    act.dma_start(batch_of(out, b - 1).rearrange("o (p t) d -> p (o t d)", t=T), o_n[1 - par][:, :]).then_inc(o_out[1 - par], 16)

        for s in (o_copy, *o_out):
            act.sem_inc(s, CREDIT)
        run(act, batch, lambda b, par: batch(b, par, 0))

    @block.vector
    def _(dve):
        dve.wait_ge(adj_in, 16)
        for t in range(T):
            dve.tensor_scalar(mask[:, t, :].rearrange("p (u q) -> p u q", u=T),
                              a_nat[:, t, :].rearrange("p (q u) -> p u q", u=T),
                              0.0, NEG, ALU.is_equal, ALU.mult).then_inc(mask_done, 1)
        dve.wait_ge(mask_done, T)

        def batch(b, par, tiles=TILES):
            first = isinstance(b, int) and b == 0
            for n in range(TILES):
                if tiles:
                    wait(dve, s_mm, CREDIT + TILES * b + n + 1)
                    wait(dve, t_mm, TILES * b + n - RING + 1)
                    settle(dve, waits_met)
                    dve.tensor_tensor_reduce(s_ring[:, n % RING, :], ps_s[n % 2][:, :], mask[:, n // HEADS, :],
                                             -SCALE, 3.0e38, ALU.add, ALU.min, low[:, n:n + 1]).then_inc(s_max, 1)
                pair = pair_after(n)
                if pair and pair[0] in DVE_PAIRS and not (first and pair[1]) and (tiles or pair[1]):
                    dst, src = copy_pair(dve, pair[0], b - pair[1], (par + pair[1]) % 2)
                    dve.tensor_copy(dst, src).then_inc(t_dve, 1)
                if n == FIN_AT and not first:
                    c, cp = b - 1, 1 - par
                    wait(dve, p_done, TILES * b)
                    dve.reciprocal(lsum[cp][:, :], lsum[cp][:, :]).then_inc(rl_done, 1)
                    wait(dve, rl_done, b)
                    wait(dve, o_mm, CREDIT + b)
                    wait(dve, o_out[cp], CREDIT + parity_count(c, cp, 16) - 16)
                    dve.tensor_tensor(o_n[cp][:, :].rearrange("p (a e) -> p a e", e=HD),
                                      ps_n[:, :].rearrange("p (a e) -> p a e", e=HD),
                                      lsum[cp][:, :].rearrange("p (a o) -> p a o", o=1).to_broadcast([128, TILES, HD]),
                                      ALU.mult).then_inc(o_div, 1)

        dve.sem_inc(o_div, CREDIT)
        run(dve, batch, lambda b, par: batch(b, par, 0))

    @block.tensor
    def _(pe):
        def transposes(n, b):
            p = n // 2
            wait(pe, p_done, TILES * b + n + 1)
            if n % 2 == 0:
                s, value = copied(p - 2, b) if p >= 2 else copied(p - 2 + PAIRS, b - 1)
                if not (isinstance(b, int) and b == 0 and p < 2):
                    wait(pe, s, value)
            for j in range(T):
                mm = pe.transpose(ps_t[p % 2][:, n % 2, j * 128:(j + 1) * 128],
                                  s_ring[:, n % RING, j * 128:(j + 1) * 128], ident[:, :])
            mm.then_inc(t_mm, 1)

        def batch(b, par, tiles=TILES):
            first = isinstance(b, int) and b == 0
            c, cp = b - 1, 1 - par
            for n in range(TILES):
                it, h = divmod(n, HEADS)
                if tiles:
                    if n == 0:
                        wait(pe, qk_in[par], parity_count(b, par, 128))
                    wait(pe, s_max, TILES * b + n - 1)
                    pe.matmul(ps_s[n % 2][:, :], q_st[par][:, h, it * 128:(it + 1) * 128],
                              k_st[par][:, h, :], start=True, stop=True).then_inc(s_mm, 1)
                if n >= LAG and tiles:
                    transposes(n - LAG, b)
                if n < LAG and not first:
                    transposes(TILES + n - LAG, c)
                if n == PV_AT and not first:
                    for p in (ACT_PAIRS[-1], DVE_PAIRS[-1]):
                        wait(pe, *copied(p, c))
                    wait(pe, v_in[cp], parity_count(c, cp, 16))
                    wait(pe, o_copy, CREDIT + c)
                    for j in range(T):
                        for hh in range(HEADS):
                            cols = slice(HD * hh, HD * (hh + 1))
                            mm = pe.matmul(ps_o[cols, :], v_sb[cp][:, j, cols], p_t[cp][:, hh, j, :],
                                           start=(j == 0), stop=(j == T - 1), tile_position=(0, HD * hh))
                    mm.then_inc(pv_mm, 1)
                if n == OT_AT and not first:
                    wait(pe, o_copy, CREDIT + b)
                    wait(pe, o_div, CREDIT + c)
                    for t in range(T):
                        mm = pe.transpose(ps_n[:, t * 128:(t + 1) * 128], o_t[:, t * 128:(t + 1) * 128], ident[:, :])
                    mm.then_inc(o_mm, 1)

        pe.sem_inc(s_mm, CREDIT)
        pe.sem_inc(pv_mm, CREDIT)
        pe.sem_inc(o_mm, CREDIT)
        run(pe, batch, lambda b, par: batch(b, par, 0))


def nothing(*_):
    pass


def graph_block(nc, x, adj, alpha, w, d, fcw, fcb, wqkv, out):
    x1_dram = nc.dram_tensor("x1_dram", [B, 128, T, D], F32, kind="Internal").ap()
    qk_dram = nc.dram_tensor("qk_dram", [B, 128, 4, N], F32, kind="Internal").ap()
    v_dram = nc.dram_tensor("v_dram", [B, 128, N], F32, kind="Internal").ap()
    with nc.sbuf_tensor("ident", [128, 128], F32) as ident:
        keep = {"ident": ident}
        with ExitStack() as kept:
            def sb(name, shape, dt=F32R):
                return kept.enter_context(nc.sbuf_tensor(name, shape, dt))
            keep["pH"] = [sb(f"pH{k}", [128, T, N]) for k in range(3)]
            keep["pL"] = [sb(f"pL{k}", [128, T, N]) for k in range(3)]
            keep["rH"], keep["rL"] = sb("rH", [128, 3, 3 * D]), sb("rL", [128, 3, 3 * D])
            keep["wH"], keep["wL"] = sb("wH", [128, 3 * D]), sb("wL", [128, 3 * D])
            keep["g"] = sb("g", [128, T, 3 * D], F32)
            with ExitStack() as ctx:
                setup_block(nc, ctx, adj, alpha, w, d, fcw, fcb, wqkv, keep)
            with ExitStack() as ctx:
                ode_block(nc, ctx, x, x1_dram, qk_dram, v_dram, keep)
        with ExitStack() as ctx:
            attention_block(nc, ctx, adj, x1_dram, qk_dram, v_dram, out, keep)


_INS = ["x", "adj", "L0_gnn_alpha_train", "L0_gnn_w", "L0_gnn_d", "L0_gnn_fc_in_w", "L0_gnn_fc_in_b", "L1_gnn_W"]


def kernel(**inputs):
    import numpy as np
    import concourse.bacc as bacc
    from concourse.bass_utils import run_bass_kernel_spmd

    nc = bacc.Bacc("TRN2", target_bir_lowering=False, num_devices=1)
    arrays, args = {}, []
    for name in _INS:
        a = np.ascontiguousarray(inputs[name])
        arrays[f"in_{name}"] = a
        args.append(nc.dram_tensor(f"in_{name}", a.shape, mybir.dt.from_np(a.dtype), kind="ExternalInput").ap())
    args.append(nc.dram_tensor("out_x", (B, N, D), F32, kind="ExternalOutput").ap())
    graph_block(nc, *args)
    r = run_bass_kernel_spmd(nc, [arrays], core_ids=[0])
    return r.results[0]["out_x"]
```

```python
from collections import namedtuple
from contextlib import ExitStack

import concourse.bass as bass
from concourse import mybir

F32 = mybir.dt.float32
F32R = mybir.dt.float32r
ALU = mybir.AluOpType
ACT = mybir.ActivationFunctionType

B, N, D = 16, 512, 128
HEADS = 4
HD = D // HEADS
T = N // 128
GB = 4
NG = B // GB
STEPS = 8
DT = 1.0 / STEPS
NC = STEPS + 1
EPS = 1e-5
NEG = -1e30
SCALE = float(HD) ** -0.5
CW = D + 1
CREDIT = 1
LOOP_BATCHES = 2


def wait(eng, sem, value):
    if isinstance(value, int) and value <= 0:
        return
    eng.wait_ge(sem, value)


def nothing(*_):
    pass


Steps = namedtuple("Steps", "u v z y ln2 back", defaults=[nothing] * 6)


def settle(eng, waits_met):
    eng.sem_inc(waits_met, 1)


def batch_of(ap, b):
    return ap[b:b + 1] if isinstance(b, int) else ap[bass.ds(b, 1)]


def split3(eng, psum, pairs, first=True, last=True):
    mm = None
    for n, ((lh, ll), (rh, rl)) in enumerate(pairs):
        eng.matmul(psum, lh, rh, start=(first and n == 0), stop=False)
        eng.matmul(psum, lh, rl, start=False, stop=False)
        mm = eng.matmul(psum, ll, rh, start=False, stop=(last and n == len(pairs) - 1))
    return mm


class Norm:

    def __init__(self, sb, sem, name, eps):
        self.eps = eps
        self.stat = sb(name + "_stat", [128, T, 6], F32)
        self.mv = sb(name + "_mv", [128, T, 2], F32)
        self.std = sb(name + "_std", [128, T], F32)
        self.st_done, self.var_done, self.std_done, self.rs_done, self.norm_done = (
            sem(f"{name}_{what}") for what in ("st_done", "var_done", "std_done", "rs_done", "norm_done"))


def norm_stats(dve, nm, n, src, tiles):
    for t in tiles:
        ins = dve.bn_stats(nm.stat[:, t, :], src(t))
        if t == T - 1:
            ins.then_inc(nm.st_done, 1)


def norm_var(dve, nm, n):
    wait(dve, nm.st_done, n + 1)
    settle(dve, nm.waits_met)
    for t in range(T):
        last = dve.bn_aggr(nm.mv[:, t, :], nm.stat[:, t, :])
    last.then_inc(nm.var_done, 1)


def norm_root(act, nm, n):
    wait(act, nm.var_done, n + 1)
    act.activation(nm.std[:, :], nm.mv[:, :, 1], ACT.Sqrt, bias=nm.eps[:, 0:1]).then_inc(nm.std_done, 1)


def norm_recip(dve, nm, n):
    wait(dve, nm.std_done, n + 1)
    dve.reciprocal(nm.std[:, :], nm.std[:, :]).then_inc(nm.rs_done, 1)
    wait(dve, nm.rs_done, n + 1)
    wait(dve, nm.var_done, n + 1)


def norm_scale(dve, nm, src, dst, tiles):
    for t in tiles:
        ins = dve.tensor_scalar(dst(t), src(t), nm.mv[:, t, 0:1], nm.std[:, t:t + 1], ALU.subtract, ALU.mult)
        if t == T - 1:
            ins.then_inc(nm.norm_done, 1)


class FirstNorm:

    def __init__(self, sb, sem):
        self.x_ln = [sb(f"x_ln{i}", [128, T, D], F32) for i in range(2)]
        self.u0 = sb("u0", [128, GB, T, D], F32)
        self.u0_h = sb("u0_h", [128, GB, T, D])
        self.u0_l = sb("u0_l", [128, GB, T, D])
        eps = sb("eps", [128, 1], F32)
        self.norm = Norm(sb, sem, "ln1", eps)
        self.waits_met = self.norm.waits_met = sem("waits_met")
        self.eps_done = sem("eps_done")
        self.xl_in = [sem(f"xl_in{i}") for i in range(2)]
        self.u0_done, self.u0h_done, self.u0l_done = sem("u0_done"), sem("u0h_done"), sem("u0l_done")
        self.u_mm = sem("u_mm")


def first_norm_load(eng, ln, x, g, b):
    wait(eng, ln.norm.norm_done, GB * g + b - 1)
    eng.dma_start(ln.x_ln[b % 2][:, :, :],
                  batch_of(x, GB * g + b).rearrange("o (p t) d -> p (o t) d", t=T)).then_inc(ln.xl_in[b % 2], 16)


def first_norm_dve(dve, ln, g, b, part):
    n = GB * g + b

    def src(t):
        return ln.x_ln[b % 2][:, t, :]

    if part == 0:
        wait(dve, ln.xl_in[b % 2], 16 * (2 * g + b // 2 + 1))
        norm_stats(dve, ln.norm, n, src, range(T))
    elif part == 1:
        norm_var(dve, ln.norm, n)
    elif part == 2:
        norm_recip(dve, ln.norm, n)
        wait(dve, ln.u_mm, 3 * (n - GB) + 3)
        wait(dve, ln.u0l_done, n - GB + 1)
        norm_scale(dve, ln.norm, src, lambda t: ln.u0[:, b, t, :], range(T // 2))
    else:
        norm_scale(dve, ln.norm, src, lambda t: ln.u0[:, b, t, :], range(T // 2, T))


def first_norm_act(act, ln, g, b):
    n = GB * g + b
    wait(act, ln.norm.norm_done, n + 1)
    act.activation(ln.u0[:, b, :, :], ln.u0[:, b, :, :], ACT.Relu).then_inc(ln.u0_done, 1)
    wait(act, ln.u0_done, n + 1)
    wait(act, ln.u_mm, 3 * (n - GB) + 3)
    act.activation(ln.u0_h[:, b, :, :], ln.u0[:, b, :, :], ACT.Copy).then_inc(ln.u0h_done, 1)


def first_norm_pool(pool, ln, g, b):
    n = GB * g + b
    wait(pool, ln.u0h_done, n + 1)
    wait(pool, ln.u_mm, 3 * (n - GB) + 3)
    pool.tensor_tensor(ln.u0_l[:, b, :, :], ln.u0[:, b, :, :], ln.u0_h[:, b, :, :].bitcast(F32),
                       ALU.subtract).then_inc(ln.u0l_done, 1)


def setup_block(nc, ctx, x, adj, alpha, w, d, fcw, fcb, wqkv, keep, ln):
    def sb(name, shape, dt=F32):
        return ctx.enter_context(nc.sbuf_tensor(name, shape, dt))

    def sem(name):
        return ctx.enter_context(nc.semaphore(name))

    a_nat = sb("a_nat", [128, T, N])
    alpha_sb = sb("alpha_sb", [128, T])
    s_col = sb("s_col", [128, T])
    e_col = sb("e_col", [128, T])
    c_col = sb("c_col", [128, T])
    w_sb = sb("w_sb", [128, D])
    d_sb = sb("d_sb", [128, 1])
    d_dt = sb("d_dt", [128, 1])
    w_qkv = sb("w_qkv", [128, 3 * D])
    p_nat = sb("p_nat", [128, T, N])
    p_h = sb("p_h", [128, T, N], F32R)
    p_l = sb("p_l", [128, T, N], F32R)
    w_t = sb("w_t", [128, D])
    w_td = sb("w_td", [128, D])
    q_sb = sb("q_sb", [128, D])
    coef = [sb(f"coef{i}", [128, NC + 1, CW]) for i in range(2)]
    pick = sb("pick", [128, 2, 3], F32R)
    s_rows = sb("s_rows", [3, N])
    c_rows = sb("c_rows", [3, 3 * D])

    ps_p = [ctx.enter_context(nc.psum_tensor(f"ps_p{i}", [128, 512], F32)) for i in range(4)]
    ps_c = ctx.enter_context(nc.psum_tensor("ps_c", [128, 3, 512], F32))
    ps_w = ctx.enter_context(nc.psum_tensor("ps_w", [128, 512], F32))

    adj_in, alpha_in, w_in, f_in, q_in = (sem(n) for n in ("adj_in", "alpha_in", "w_in", "f_in", "q_in"))
    exp_done, col_done, ident_done, coef_zero = (sem(n) for n in ("exp_done", "col_done", "ident_done", "coef_zero"))
    p_done, ph_done, pl_done = (sem(n) for n in ("p_done", "ph_done", "pl_done"))
    pow_mm, pow_h, pow_l = (sem(n) for n in ("pow_mm", "pow_h", "pow_l"))
    w_mm, w_done = sem("w_mm"), sem("w_done")
    coef_mm, coef_done, coef_ready = sem("coef_mm"), sem("coef_done"), sem("coef_ready")
    r_mm, r_h, r_l = sem("r_mm"), sem("r_h"), sem("r_l")
    row_mm, row_done, g_mm, g_done = (sem(n) for n in ("row_mm", "row_done", "g_mm", "g_done"))
    qw_h, qw_l, pick_done = sem("qw_h"), sem("qw_l"), sem("pick_done")

    ident = keep["ident"]
    block = ctx.enter_context(nc.Block())

    @block.sync
    def _(sp):
        sp.dma_start(a_nat[:, :, :], adj.rearrange("(p t) m -> p t m", t=T)).then_inc(adj_in, 16)
        for b in range(GB):
            first_norm_load(sp, ln, x, 0, b)
            if b == 1:
                sp.dma_start(w_qkv[:, :], wqkv).then_inc(q_in, 16)

    @block.gpsimd
    def _(pool):
        pool.memset(ident[:, :], 0.0).then_inc(ident_done, 1)
        pool.wait_ge(ident_done, 1)
        pool.affine_select(out=ident[:, :], in_=ident[:, :], compare_op=ALU.not_equal, fill=1.0,
                           base=0, pattern=[[-1, 128]], channel_multiplier=1).then_inc(ident_done, 1)
        for c in coef:
            pool.memset(c[:, :, :], 0.0).then_inc(coef_zero, 1)
        pool.memset(pick[:, :, :].bitcast(F32), 0.0).then_inc(pick_done, 1)
        pool.wait_ge(pick_done, 1)
        for j in range(2):
            pool.memset(pick[:, j, j + 1:j + 2].bitcast(F32), 1.0).then_inc(pick_done, 1)
        pool.memset(ln.norm.eps[:, :], EPS).then_inc(ln.eps_done, 1)
        for b in range(GB):
            first_norm_pool(pool, ln, 0, b)

    @block.scalar
    def _(act):
        act.dma_start(alpha_sb[:, :], alpha.rearrange("(p t) -> p t", t=T)).then_inc(alpha_in, 16)
        act.dma_start(w_sb[:, :], w).then_inc(w_in, 16)
        act.dma_start(d_sb[:, :], d.rearrange("(p o) -> p o", o=1)).then_inc(w_in, 16)
        act.wait_ge(coef_zero, 2)
        act.dma_start(coef[0][:, 1, 0:D], fcw).then_inc(f_in, 16)
        act.dma_start(coef[0][:, 1, D:CW], fcb.rearrange("(p o) -> p o", o=1)).then_inc(f_in, 16)
        act.wait_ge(alpha_in, 16)
        act.activation(e_col[:, :], alpha_sb[:, :], ACT.Exp, scale=-1.0).then_inc(exp_done, 1)
        act.wait_ge(q_in, 16)
        act.activation(keep["wH"][:, :], w_qkv[:, :], ACT.Copy).then_inc(qw_h, 1)
        for t in range(T):
            act.wait_ge(p_done, t + 1)
            act.activation(p_h[:, t, :], p_nat[:, t, :], ACT.Copy).then_inc(ph_done, 1)
        for k in range(3):
            for m in range(T):
                act.wait_ge(pow_mm, k * T + m + 1)
                act.activation(keep["pH"][k][:, m, :], ps_p[m][:, :], ACT.Copy).then_inc(pow_h, 1)
                n = (k - 1) * T + m
                if n == 0:
                    act.wait_ge(ln.eps_done, 1)
                if k >= 1 and n % 2 == 0:
                    norm_root(act, ln.norm, n // 2)
                elif k >= 1:
                    first_norm_act(act, ln, 0, n // 2)
        for j in range(3):
            act.wait_ge(r_mm, j + 1)
            act.activation(keep["rH"][:, j, :], ps_p[j][:, 0:3 * D], ACT.Copy).then_inc(r_h, 1)
        act.wait_ge(row_mm, 1)
        act.activation(c_rows[:, :], ps_p[3][0:3, 0:3 * D], ACT.Copy).then_inc(row_done, 1)
        for t in range(T):
            act.wait_ge(g_mm, t + 1)
            act.activation(keep["g"][:, t, :], ps_p[t][:, 0:3 * D], ACT.Copy).then_inc(g_done, 1)

    @block.vector
    def _(dve):
        n_col = 0

        def col(ins):
            nonlocal n_col
            n_col += 1
            ins.then_inc(col_done, 1)
            dve.wait_ge(col_done, n_col)

        dve.wait_ge(exp_done, 1)
        col(dve.tensor_scalar(e_col[:, :], e_col[:, :], 1.0, None, ALU.add))
        col(dve.reciprocal(s_col[:, :], e_col[:, :]))
        col(dve.tensor_scalar(s_col[:, :], s_col[:, :], 0.5 * DT, None, ALU.mult))
        col(dve.tensor_scalar(c_col[:, :], s_col[:, :], -1.0, 1.0 - DT, ALU.mult, ALU.add))
        dve.wait_ge(adj_in, 16)
        dve.wait_ge(ident_done, 2)
        for t in range(T):
            dst = p_nat[:, t, :].rearrange("p (u q) -> p u q", u=T)
            src = a_nat[:, t, :].rearrange("p (q u) -> p u q", u=T)
            col(dve.tensor_scalar(dst, src, s_col[:, t:t + 1], None, ALU.mult))
            diag = p_nat[:, t, t * 128:(t + 1) * 128]
            dve.scalar_tensor_tensor(out=diag, in0=ident[:, :], scalar=c_col[:, t:t + 1], in1=diag,
                                     op0=ALU.mult, op1=ALU.add).then_inc(p_done, 1)
        dve.wait_ge(w_in, 32)
        col(dve.tensor_scalar(d_dt[:, :], d_sb[:, :], 0.0, 1.0, ALU.max, ALU.min))
        col(dve.tensor_scalar(d_dt[:, :], d_dt[:, :], DT, None, ALU.mult))
        dve.wait_ge(w_mm, 1)
        dve.tensor_copy(w_t[:, :], ps_w[:, 0:D])
        dve.tensor_scalar(w_td[:, :], ps_w[:, 0:D], d_dt[:, 0:1], None, ALU.mult).then_inc(w_done, 1)
        dve.wait_ge(w_mm, 2)
        dve.tensor_copy(q_sb[:, :], ps_w[:, 0:D]).then_inc(w_done, 1)
        dve.wait_ge(coef_zero, 2)
        for c in coef:
            dve.tensor_scalar(c[:, 0, 0:D], ident[:, :], DT, None, ALU.mult).then_inc(coef_ready, 1)
        dve.wait_ge(coef_ready, 2)
        dve.wait_ge(f_in, 32)

        def low(i):
            if i < T:
                dve.wait_ge(ph_done, i + 1)
                dve.tensor_tensor(p_l[:, i, :], p_nat[:, i, :], p_h[:, i, :].bitcast(F32),
                                  ALU.subtract).then_inc(pl_done, 1)
            else:
                k, m = divmod(i - T, T)
                dve.wait_ge(pow_h, k * T + m + 1)
                dve.tensor_tensor(keep["pL"][k][:, m, :], ps_p[m][:, :], keep["pH"][k][:, m, :].bitcast(F32),
                                  ALU.subtract).then_inc(pow_l, 1)

        def step(n):
            old, new = coef[n % 2], coef[(n + 1) % 2]
            if n:
                dve.wait_ge(coef_done, n)
            dve.tensor_copy(new[:, n + 2, :], old[:, n + 1, :])
            dve.wait_ge(coef_mm, n + 1)
            for s in range(1, n + 2, 3):
                k = min(3, n + 2 - s)
                last = dve.tensor_tensor(new[:, s:s + k, :],
                                         ps_c[:, (s - 1) // 3, 0:k * CW].rearrange("p (k c) -> p k c", c=CW),
                                         old[:, s - 1:s - 1 + k, :], ALU.add)
            last.then_inc(coef_done, 1)

        for i in range(2 * T):
            low(i)
        for n in range(STEPS):
            if n % 2 == 0:
                first_norm_dve(dve, ln, 0, n // 2, 0)
                first_norm_dve(dve, ln, 0, n // 2, 1)
            step(n)
            low(2 * T + n)
            if n % 2:
                first_norm_dve(dve, ln, 0, n // 2, 2)
                first_norm_dve(dve, ln, 0, n // 2, 3)
        dve.wait_ge(qw_h, 1)
        dve.tensor_tensor(keep["wL"][:, :], w_qkv[:, :], keep["wH"][:, :].bitcast(F32),
                          ALU.subtract).then_inc(qw_l, 1)
        for j in range(3):
            dve.wait_ge(r_h, j + 1)
            dve.tensor_tensor(keep["rL"][:, j, :], ps_p[j][:, 0:3 * D], keep["rH"][:, j, :].bitcast(F32),
                              ALU.subtract).then_inc(r_l, 1)
        dve.wait_ge(row_mm, 2)
        dve.tensor_scalar(s_rows[:, :], ps_w[0:3, :], ident[0:3, 0:1], None, ALU.add).then_inc(row_done, 1)

    @block.tensor
    def _(pe):
        pe.wait_ge(ident_done, 2)
        pe.wait_ge(w_in, 32)
        pe.transpose(ps_w[:, 0:D], w_sb[:, :], ident[:, :]).then_inc(w_mm, 1)
        pe.wait_ge(w_done, 1)
        pe.matmul(ps_w[:, 0:D], w_td[:, :], w_t[:, :], start=True, stop=True).then_inc(w_mm, 1)
        pe.wait_ge(p_done, T)
        for m in range(T):
            for t in range(T):
                tr = pe.transpose(ps_p[m][:, t * 128:(t + 1) * 128], p_nat[:, t, m * 128:(m + 1) * 128], ident[:, :])
            tr.then_inc(pow_mm, 1)
        pe.wait_ge(w_done, 2)
        pe.wait_ge(f_in, 32)
        pe.wait_ge(coef_zero, 2)
        pe.wait_ge(coef_ready, 2)

        def power(k, m):
            if m == 0:
                pe.wait_ge(pow_l, k * T)
                pe.wait_ge(ph_done, T)
                pe.wait_ge(pl_done, T)
            pairs = [((p_h[:, c, m * 128:(m + 1) * 128], p_l[:, c, m * 128:(m + 1) * 128]),
                      (keep["pH"][k - 1][:, c, :], keep["pL"][k - 1][:, c, :])) for c in range(T)]
            split3(pe, ps_p[m][:, :], pairs).then_inc(pow_mm, 1)

        for n in range(STEPS):
            if n:
                pe.wait_ge(coef_done, n)
            for s in range(1, n + 2, 3):
                k = min(3, n + 2 - s)
                mm = pe.matmul(ps_c[:, (s - 1) // 3, 0:k * CW], q_sb[:, :],
                               coef[n % 2][:, s:s + k, :].rearrange("p k c -> p (k c)"), start=True, stop=True)
            mm.then_inc(coef_mm, 1)
            power(1 + n // T, n % T)
        fin = coef[STEPS % 2]
        pe.wait_ge(coef_done, STEPS)
        pe.wait_ge(pow_l, 3 * T)
        for j in range(3):
            for i in range(3):
                tr = pe.transpose(ps_p[j][:, i * D:(i + 1) * D], fin[:, 1 + 3 * i + j, 0:D], ident[:, :])
            tr.then_inc(r_mm, 1)
        for i in range(3):
            tr = pe.transpose(ps_p[3][0:3, i * D:(i + 1) * D], fin[:, 1 + 3 * i:4 + 3 * i, D], ident[:, :])
        tr.then_inc(row_mm, 1)
        pe.wait_ge(pick_done, 3)
        for j in range(2):
            for m in range(T):
                for part in ("pH", "pL"):
                    mm = pe.matmul(ps_w[0:3, :], pick[:, j, :], keep[part][j][:, m, :],
                                   start=(j == 0 and m == 0 and part == "pH"),
                                   stop=(j == 1 and m == T - 1 and part == "pL"))
        mm.then_inc(row_mm, 1)
        pe.wait_ge(row_done, 2)
        pe.wait_ge(r_l, 3)
        for t in range(T):
            pe.matmul(ps_p[t][:, 0:3 * D], s_rows[:, t * 128:(t + 1) * 128], c_rows[:, :],
                      start=True, stop=True).then_inc(g_mm, 1)


def ode_block(nc, ctx, x, x1_dram, qk_dram, v_dram, keep, ln):
    def sb(name, shape, dt=F32):
        return ctx.enter_context(nc.sbuf_tensor(name, shape, dt))

    def sem(name):
        return ctx.enter_context(nc.semaphore(name))

    def bank(name):
        return ctx.enter_context(nc.psum_tensor(name, [128, 512], F32))

    x_res = sb("x_res", [128, T, D])
    ut_h = [sb(f"ut_h{i}", [128, 3, N], F32R) for i in range(2)]
    ut_l = [sb(f"ut_l{i}", [128, 3, N], F32R) for i in range(2)]
    v = sb("v", [128, T, GB, 3 * D])
    v2_h = sb("v2_h", [128, T, GB, D], F32R)
    v2_l = sb("v2_l", [128, T, GB, D], F32R)
    z_h = sb("z_h", [128, T, GB, D], F32R)
    z_l = sb("z_l", [128, T, GB, D], F32R)
    h2 = sb("h2", [128, GB, T, D])
    ht_h = [sb(f"ht_h{i}", [128, N], F32R) for i in range(2)]
    ht_l = [sb(f"ht_l{i}", [128, N], F32R) for i in range(2)]
    qk = [sb(f"qk{i}", [128, 2, N], F32R) for i in range(2)]
    vt = [sb(f"vt{i}", [128, N]) for i in range(2)]
    v_nat = sb("v_nat", [128, N])
    ln2n = Norm(sb, sem, "ln2", ln.norm.eps)

    ps_u = [bank(f"ps_u{i}") for i in range(2)]
    ps_v = [bank(f"ps_v{i}") for i in range(2)]
    ps_z = [bank(f"ps_z{i}") for i in range(2)]
    ps_k = [bank(f"ps_k{i}") for i in range(2)]

    ident = keep["ident"]
    waits_met = ln.waits_met
    ln2n.waits_met = waits_met
    u0, u0_h, u0_l, u0_done, u0l_done = ln.u0, ln.u0_h, ln.u0_l, ln.u0_done, ln.u0l_done
    xr_in = sem("xr_in")
    u_mm, uh_done, ul_done = ln.u_mm, sem("uh_done"), sem("ul_done")
    v_mm, v_add, v2h_done, v2l_done, xv_done = (sem(n) for n in ("v_mm", "v_add", "v2h_done", "v2l_done", "xv_done"))
    z_mm, z_add, zh_done, zl_done = (sem(n) for n in ("z_mm", "z_add", "zh_done", "zl_done"))
    y_mm, x1_add, x1_out = sem("y_mm"), sem("x1_add"), sem("x1_out")
    h2_done = sem("h2_done")
    k_mm, kh_done, kl_done, vt_done, vn_done = (sem(n) for n in ("k_mm", "kh_done", "kl_done", "vt_done", "vn_done"))
    qk_out = [sem(f"qk_out{i}") for i in range(2)]
    v_out = sem("v_out")

    BACK = [("t", 0), ("t", 1), ("q", 0), ("k", 0), ("vt", 0), ("q", 1), ("k", 1), ("vt", 1), ("v", 0), ("v", 1)]
    NB = len(BACK)
    SPLIT = [i for i, (kind, _) in enumerate(BACK) if kind in "tqk"]
    VT = [i for i, (kind, _) in enumerate(BACK) if kind == "vt"]
    VN = [i for i, (kind, _) in enumerate(BACK) if kind == "v"]

    def freed(i, pair):
        if i in SPLIT:
            return kl_done, len(SPLIT) * pair + SPLIT.index(i) + 1
        if i in VT:
            return vt_done, len(VT) * pair + VT.index(i) + 1
        return vn_done, len(VN) * pair + VN.index(i) + 1

    def group(g, steps, prev=True, following=True):
        def back(pair, lo, hi):
            if prev:
                steps.back(g - 1, pair, lo, hi)
        steps.u(g, 0, prev)
        for b in range(1, GB):
            steps.u(g, b, prev)
            steps.v(g, b - 1, following)
        back(0, 0, 2)
        steps.v(g, GB - 1, following)
        back(0, 2, 8)
        for t in range(T):
            steps.z(g, t)
            if t < 2:
                back(0, 8 + t, 9 + t)
            if t == 2:
                back(1, 0, 2)
        back(1, 2, 8)
        for t in range(T):
            steps.y(g, t)
            if t < 2:
                back(1, 8 + t, 9 + t)

    def run(eng, steps):
        group(0, steps, prev=False)
        with eng.Fori(1, NG - 1) as g:
            group(g, steps)
        group(NG - 1, steps, following=False)
        for b in range(GB):
            steps.ln2(NG - 1, b)
        for pair in range(2):
            steps.back(NG - 1, pair, 0, NB)

    block = ctx.enter_context(nc.Block())

    @block.sync
    def _(sp):
        def u_step(g, b, prev):
            if b == 0 and prev:
                store_x1(g - 1)

        def v_step(g, b, following):
            if following:
                first_norm_load(sp, ln, x, g + 1, b)
            wait(sp, xv_done, GB * g + b)
            sp.dma_start(x_res[:, :, :], batch_of(x, GB * g + b).rearrange("o (p t) d -> p (o t) d", t=T)).then_inc(xr_in, 16)

        def store_x1(g):
            wait(sp, x1_add, T * (g + 1))
            for c in range(GB):
                sp.dma_start(batch_of(x1_dram, GB * g + c).rearrange("o p t d -> p (o t) d"), v[:, :, c, 0:D]).then_inc(x1_out, 16)

        def ln2(g, b):
            if b == 0:
                store_x1(g)

        def back(g, pair, lo, hi):
            for i, (kind, c) in list(enumerate(BACK))[lo:hi]:
                b = 2 * pair + c
                if kind in ("q", "k"):
                    which = 0 if kind == "q" else 1
                    wait(sp, kl_done, len(SPLIT) * (2 * g + pair) + SPLIT.index(i) + 1)
                    dst = batch_of(qk_dram, GB * g + b)[:, :, 2 * which:2 * which + 2, :].rearrange("o p s n -> p (o s) n")
                    sp.dma_start(dst, qk[which][:, :, :].bitcast(F32)).then_inc(qk_out[which], 16)
                if kind == "v":
                    wait(sp, vn_done, 2 * (2 * g + pair) + c + 1)
                    sp.dma_start(batch_of(v_dram, GB * g + b).rearrange("o p n -> p (o n)"), v_nat[:, :]).then_inc(v_out, 16)

        for s in (*qk_out, v_out):
            sp.sem_inc(s, CREDIT)
        run(sp, Steps(u=u_step, v=v_step, ln2=ln2, back=back))
        sp.wait_ge(x1_out, 16 * B)
        for s in (*qk_out, v_out):
            sp.wait_ge(s, CREDIT + 16 * B)

    @block.gpsimd
    def _(pool):
        def v_step(g, b, following):
            n = GB * g + b
            wait(pool, v2h_done, n + 1)
            wait(pool, z_mm, T * g)
            pool.tensor_tensor(v2_l[:, :, b, :], v[:, :, b, 2 * D:3 * D], v2_h[:, :, b, :].bitcast(F32),
                               ALU.subtract).then_inc(v2l_done, 1)
            wait(pool, xr_in, 16 * (n + 1))
            wait(pool, v_add, T * (n + 1))
            pool.tensor_tensor(v[:, :, b, 0:D], v[:, :, b, 0:D], x_res[:, :, :], ALU.add).then_inc(xv_done, 1)
            if following:
                first_norm_pool(pool, ln, g + 1, b)

        def z_step(g, t):
            wait(pool, zh_done, T * g + t + 1)
            wait(pool, y_mm, T * g)
            pool.tensor_tensor(z_l[:, t, :, :], v[:, t, :, D:2 * D], z_h[:, t, :, :].bitcast(F32),
                               ALU.subtract).then_inc(zl_done, 1)

        run(pool, Steps(v=v_step, z=z_step))

    @block.scalar
    def _(act):
        def u_step(g, b, prev):
            for k in range(3):
                n = 3 * (GB * g + b) + k
                wait(act, u_mm, n + 1)
                wait(act, v_mm, T * (GB * g + b - 1))
                act.activation(ut_h[b % 2][:, k, :], ps_u[(3 * b + k) % 2][:, :], ACT.Copy).then_inc(uh_done, 1)
                if k == 0 and prev:
                    norm_root(act, ln2n, GB * (g - 1) + b)
                if k == 1 and prev:
                    relu(g - 1, b)

        def relu(g, b):
            n = GB * g + b
            wait(act, ln2n.norm_done, n + 1)
            act.activation(h2[:, b, :, :], h2[:, b, :, :], ACT.Relu).then_inc(h2_done, 1)

        def ln2(g, b):
            norm_root(act, ln2n, GB * g + b)
            relu(g, b)

        def v_step(g, b, following):
            n = GB * g + b
            if following:
                norm_root(act, ln.norm, n + GB)
            wait(act, v_add, T * (n + 1))
            wait(act, z_mm, T * g)
            act.activation(v2_h[:, :, b, :], v[:, :, b, 2 * D:3 * D], ACT.Copy).then_inc(v2h_done, 1)
            if following:
                first_norm_act(act, ln, g + 1, b)

        def z_step(g, t):
            wait(act, z_add, T * g + t + 1)
            wait(act, y_mm, T * g)
            act.activation(z_h[:, t, :, :], v[:, t, :, D:2 * D], ACT.Copy).then_inc(zh_done, 1)

        def back(g, pair, lo, hi):
            pr = 2 * g + pair
            for i, (kind, c) in list(enumerate(BACK))[lo:hi]:
                wait(act, k_mm, NB * pr + i + 1)
                src = ps_k[i % 2][:, :]
                if kind == "t":
                    if pair:
                        wait(act, k_mm, NB * (pr - 1) + VT[c] + 1)
                    act.activation(ht_h[c][:, :], src, ACT.Copy).then_inc(kh_done, 1)
                elif kind in ("q", "k"):
                    which = 0 if kind == "q" else 1
                    wait(act, qk_out[which], CREDIT + 16 * (2 * pr + c))
                    act.activation(qk[which][:, 0, :], src, ACT.Copy).then_inc(kh_done, 1)
                elif kind == "vt":
                    if pair:
                        wait(act, k_mm, NB * (pr - 1) + VN[c] + 1)
                    act.activation(vt[c][:, :], src, ACT.Copy).then_inc(vt_done, 1)
                else:
                    wait(act, v_out, CREDIT + 16 * (2 * pr + c))
                    act.activation(v_nat[:, :], src, ACT.Copy).then_inc(vn_done, 1)

        run(act, Steps(u=u_step, v=v_step, ln2=ln2, back=back, z=z_step))

    @block.vector
    def _(dve):
        def x1_rows(b):
            return lambda t: v[:, t, b, 0:D]

        def u_step(g, b, prev):
            for k in range(3):
                n = 3 * (GB * g + b) + k
                wait(dve, uh_done, n + 1)
                wait(dve, v_mm, T * (GB * g + b - 1))
                dve.tensor_tensor(ut_l[b % 2][:, k, :], ps_u[(3 * b + k) % 2][:, :],
                                  ut_h[b % 2][:, k, :].bitcast(F32), ALU.subtract).then_inc(ul_done, 1)
                if k == 0 and prev:
                    wait(dve, x1_add, T * g)
                    norm_stats(dve, ln2n, GB * (g - 1) + b, x1_rows(b), range(T))
                    norm_var(dve, ln2n, GB * (g - 1) + b)
                if k == 1 and prev:
                    scale_h2(g - 1, b)

        def scale_h2(g, b):
            norm_recip(dve, ln2n, GB * g + b)
            norm_scale(dve, ln2n, x1_rows(b), lambda t: h2[:, b, t, :], range(T))

        def ln2(g, b):
            wait(dve, x1_add, T * (g + 1))
            norm_stats(dve, ln2n, GB * g + b, x1_rows(b), range(T))
            norm_var(dve, ln2n, GB * g + b)
            scale_h2(g, b)

        def v_step(g, b, following):
            for t in range(T):
                n = T * (GB * g + b) + t
                wait(dve, v_mm, n + 1)
                if t == 0:
                    wait(dve, x1_out, 16 * GB * g)
                    wait(dve, ln2n.norm_done, GB * (g - 1) + b + 1)
                    wait(dve, zl_done, T * g)
                    wait(dve, v2l_done, GB * (g - 1) + b + 1)
                dve.tensor_tensor(v[:, t, b, :], ps_v[t % 2][:, 0:3 * D], keep["g"][:, t, :],
                                  ALU.add).then_inc(v_add, 1)
                if following:
                    first_norm_dve(dve, ln, g + 1, b, t)

        def z_step(g, t):
            wait(dve, z_mm, T * g + t + 1)
            wait(dve, v_add, T * GB * (g + 1))
            dve.tensor_tensor(v[:, t, :, D:2 * D], ps_z[t % 2][:, :].rearrange("p (b d) -> p b d", b=GB),
                              v[:, t, :, D:2 * D], ALU.add).then_inc(z_add, 1)

        def y_step(g, t):
            wait(dve, y_mm, T * g + t + 1)
            wait(dve, xv_done, GB * (g + 1))
            dve.tensor_tensor(v[:, t, :, 0:D], ps_z[t % 2][:, :].rearrange("p (b d) -> p b d", b=GB),
                              v[:, t, :, 0:D], ALU.add).then_inc(x1_add, 1)

        def back(g, pair, lo, hi):
            pr = 2 * g + pair
            for i, (kind, c) in list(enumerate(BACK))[lo:hi]:
                if i not in SPLIT:
                    continue
                wait(dve, kh_done, len(SPLIT) * pr + SPLIT.index(i) + 1)
                src = ps_k[i % 2][:, :]
                if kind == "t":
                    if pair:
                        wait(dve, k_mm, NB * (pr - 1) + VT[c] + 1)
                    dst, high = ht_l[c][:, :], ht_h[c][:, :]
                else:
                    which = 0 if kind == "q" else 1
                    wait(dve, qk_out[which], CREDIT + 16 * (2 * pr + c))
                    dst, high = qk[which][:, 1, :], qk[which][:, 0, :]
                dve.tensor_tensor(dst, src, high.bitcast(F32), ALU.subtract).then_inc(kl_done, 1)

        run(dve, Steps(u=u_step, v=v_step, ln2=ln2, back=back, z=z_step, y=y_step))

    @block.tensor
    def _(pe):
        def u_step(g, b, prev):
            nb = GB * g + b
            for k in range(3):
                n = 3 * nb + k
                wait(pe, ul_done, n - 1)
                ps = ps_u[(3 * b + k) % 2]
                if k == 0:
                    wait(pe, u0_done, nb + 1)
                    for t in range(T):
                        mm = pe.transpose(ps[:, t * 128:(t + 1) * 128], u0[:, b, t, :], ident[:, :])
                else:
                    wait(pe, u0l_done, nb + 1)
                    mm = split3(pe, ps[:, :], [((u0_h[:, b, m, :], u0_l[:, b, m, :]),
                                                (keep["pH"][k - 1][:, m, :], keep["pL"][k - 1][:, m, :]))
                                               for m in range(T)])
                mm.then_inc(u_mm, 1)

        def v_step(g, b, following):
            nb = GB * g + b
            wait(pe, ul_done, 3 * nb + 3)
            for t in range(T):
                wait(pe, v_add, T * nb + t - 1)
                rows = slice(t * 128, (t + 1) * 128)
                split3(pe, ps_v[t % 2][:, 0:3 * D], [((ut_h[b % 2][:, k, rows], ut_l[b % 2][:, k, rows]),
                                                     (keep["rH"][:, k, :], keep["rL"][:, k, :]))
                                                    for k in range(3)]).then_inc(v_mm, 1)

        def cube(g, t, src_h, src_l):
            rows = slice(t * 128, (t + 1) * 128)
            return split3(pe, ps_z[t % 2][:, :],
                          [((keep["pH"][2][:, m, rows], keep["pL"][2][:, m, rows]),
                            (src_h[:, m, :, :].rearrange("p b d -> p (b d)"),
                             src_l[:, m, :, :].rearrange("p b d -> p (b d)"))) for m in range(T)])

        def z_step(g, t):
            if t == 0:
                wait(pe, v2l_done, GB * (g + 1))
            if t < 2:
                wait(pe, x1_add, T * g - 2 + t + 1)
            else:
                wait(pe, z_add, T * g + t - 1)
            cube(g, t, v2_h, v2_l).then_inc(z_mm, 1)

        def y_step(g, t):
            if t == 0:
                wait(pe, zl_done, T * (g + 1))
            if t < 2:
                wait(pe, z_add, T * g + 2 + t + 1)
            else:
                wait(pe, x1_add, T * g + t - 1)
            cube(g, t, z_h, z_l).then_inc(y_mm, 1)

        def back(g, pair, lo, hi):
            pr = 2 * g + pair
            for i, (kind, c) in list(enumerate(BACK))[lo:hi]:
                ps = ps_k[i % 2]
                if i >= 2:
                    wait(pe, *freed(i - 2, pr))
                elif pair:
                    wait(pe, *freed(NB + i - 2, pr - 1))
                if kind == "t":
                    b = 2 * pair + c
                    wait(pe, h2_done, GB * g + b + 1)
                    for t in range(T):
                        mm = pe.transpose(ps[:, t * 128:(t + 1) * 128], h2[:, b, t, :], ident[:, :])
                elif kind == "v":
                    wait(pe, vt_done, 2 * pr + c + 1)
                    for t in range(T):
                        mm = pe.transpose(ps[:, t * 128:(t + 1) * 128], vt[c][:, t * 128:(t + 1) * 128], ident[:, :])
                else:
                    wait(pe, kl_done, len(SPLIT) * pr + c + 1)
                    at = {"q": 0, "k": D, "vt": 2 * D}[kind]
                    mm = split3(pe, ps[:, :], [((keep["wH"][:, at:at + D], keep["wL"][:, at:at + D]),
                                                (ht_h[c][:, :], ht_l[c][:, :]))])
                mm.then_inc(k_mm, 1)

        run(pe, Steps(u=u_step, v=v_step, back=back, z=z_step, y=y_step))


def attention_block(nc, ctx, adj, x1_dram, qk_dram, v_dram, out, keep):
    def sb(name, shape, dt=F32):
        return ctx.enter_context(nc.sbuf_tensor(name, shape, dt))

    def sem(name):
        return ctx.enter_context(nc.semaphore(name))

    TILES = T * HEADS
    PAIRS = TILES // 2
    RING = 8
    LAG = 4
    ACT_PAIRS = [1, 3, 5, 7]
    DVE_PAIRS = [p for p in range(PAIRS) if p not in ACT_PAIRS]
    COPY_BEFORE = [6, 6, 10, 12, 14, 15, 18, 18]
    PV_AT = {5: 2, 6: 1, 7: 1, 9: 3, 10: 1, 11: 2, 12: 2, 13: 4}
    OCOPY_AT, OT_AT, FIN_AT = 13, 15, 15
    assert sum(PV_AT.values()) == HEADS * T
    PV_RANGE = [(sum(PV_AT.get(i, 0) for i in range(n)), sum(PV_AT.get(i, 0) for i in range(n + 1))) for n in range(TILES)]
    S_BANKS = 3
    S_BANK = [n % S_BANKS for n in range(TILES - 1)] + [1]
    S_BACK = [next(k for k in range(1, TILES) if S_BANK[n - k] == S_BANK[n]) for n in range(TILES)]

    a_nat = sb("a_nat2", [128, T, N])
    mask = sb("mask", [128, T, N])
    q_st = [sb(f"q_st{i}", [128, HEADS, N], F32R) for i in range(2)]
    k_st = [sb(f"k_st{i}", [128, HEADS, N], F32R) for i in range(2)]
    v_sb = [sb(f"v_sb{i}", [128, T, D]) for i in range(2)]
    x1 = [sb(f"x1_{i}", [128, T * D]) for i in range(2)]
    s_ring = sb("s_ring", [128, RING, N])
    low = sb("low", [128, TILES])
    lsum = [sb(f"lsum{i}", [128, TILES]) for i in range(2)]
    p_t = [sb(f"p_t{i}", [128, HEADS, T, N]) for i in range(2)]
    o_t = sb("o_t", [128, N])
    o_n = [sb(f"o_n{i}", [128, T * D]) for i in range(2)]

    ps_s = [ctx.enter_context(nc.psum_tensor(f"ps_s{i}", [128, N], F32)) for i in range(S_BANKS)]
    ps_t = [ctx.enter_context(nc.psum_tensor(f"ps_t{i}", [128, 2, N], F32)) for i in range(2)]
    ps_o = ctx.enter_context(nc.psum_tensor("ps_o", [128, N], F32))
    ps_n = ps_o

    ident = keep["ident"]
    adj_in, mask_done, waits_met = sem("adj2_in"), sem("mask_done"), sem("waits_met2")
    qk_in = [sem(f"qk_in{i}") for i in range(2)]
    v_in = [sem(f"v_in{i}") for i in range(2)]
    x_in = [sem(f"x_in{i}") for i in range(2)]
    s_mm, s_max, p_done, t_mm, t_act, t_dve = (sem(n) for n in ("s_mm", "s_max", "p_done", "t_mm", "t_act", "t_dve"))
    pv_mm, o_copy, o_mm, rl_done, o_div, o_add = (sem(n) for n in ("pv_mm", "o_copy", "o_mm", "rl_done", "o_div", "o_add"))
    o_out = [sem(f"o_out{i}") for i in range(2)]

    def run(eng, batch, tail):
        batch(0, 0)
        with eng.Fori(0, (B - 2) // LOOP_BATCHES) as turn:
            for k in range(LOOP_BATCHES):
                batch(turn * LOOP_BATCHES + (1 + k), (1 + k) % 2)
        batch(B - 1, (B - 1) % 2)
        tail(B, B % 2)

    def copied(p, b):
        if p in ACT_PAIRS:
            return t_act, len(ACT_PAIRS) * b + ACT_PAIRS.index(p) + 1
        return t_dve, len(DVE_PAIRS) * b + DVE_PAIRS.index(p) + 1

    def pairs_before(n, mine):
        return [(p, COPY_BEFORE[p] // TILES) for p in mine if COPY_BEFORE[p] % TILES == n]

    def copy_pair(eng, p, b, par):
        wait(eng, t_mm, TILES * b + 2 * p + 2)
        if p in (ACT_PAIRS[0], DVE_PAIRS[0]):
            wait(eng, pv_mm, CREDIT + b - 1)
        it, h = divmod(2 * p, HEADS)
        dst = p_t[par][:, h:h + 2, :, it * 128:(it + 1) * 128]
        src = ps_t[p % 2][:, :, :].rearrange("p h (j i) -> p h j i", j=T)
        return dst, src

    block = ctx.enter_context(nc.Block())

    @block.sync
    def _(sp):
        sp.dma_start(a_nat[:, :, :], adj.rearrange("(p t) m -> p t m", t=T)).then_inc(adj_in, 16)

        def load(b, par):
            src = batch_of(qk_dram, b)
            wait(sp, s_mm, CREDIT + TILES * (b - 1))
            for slot in range(4):
                for st, part in ((q_st, slot // 2), (k_st, 2 + slot % 2)):
                    sp.dma_start(st[par][HD * slot:HD * (slot + 1), :, :].bitcast(F32),
                                 src[:, :, part:part + 1, :].rearrange("o (h e) s n -> e (o s h) n", e=HD)).then_inc(qk_in[par], 16)
            wait(sp, pv_mm, CREDIT + b - 1)
            sp.dma_start(v_sb[par][:, :, :].rearrange("p t d -> p (t d)"), batch_of(v_dram, b).rearrange("o p n -> p (o n)")).then_inc(v_in[par], 16)
            wait(sp, o_add, CREDIT + b - 1)
            sp.dma_start(x1[par][:, :], batch_of(x1_dram, b).rearrange("o p t d -> p (o t d)")).then_inc(x_in[par], 16)

        def batch(b, par):
            first, last = (isinstance(b, int) and b == n for n in (0, B - 1))
            if not last:
                load(b + 1, 1 - par)
            if not first:
                store(b - 1, 1 - par)

        def store(b, par):
            wait(sp, o_add, CREDIT + b + 1)
            sp.dma_start(batch_of(out, b).rearrange("o (p t) d -> p (o t d)", t=T), o_n[par][:, :]).then_inc(o_out[par], 16)

        for s in o_out:
            sp.sem_inc(s, CREDIT)
        load(0, 0)
        run(sp, batch, lambda b, par: store(b - 1, 1 - par))
        for s in o_out:
            sp.wait_ge(s, CREDIT + 16 * B // 2)

    def parity_count(b, par, each):
        if isinstance(b, int):
            return each * (b // 2 + 1)
        assert each % 2 == 0
        return b * (each // 2) + (each // 2) * (2 - par)

    @block.gpsimd
    def _(pool):
        def batch(b, par):
            if isinstance(b, int) and b == 0:
                return
            c, cp = b - 1, 1 - par
            wait(pool, o_div, CREDIT + c + 1)
            wait(pool, x_in[cp], parity_count(c, cp, 16))
            pool.tensor_tensor(o_n[cp][:, :], o_n[cp][:, :], x1[cp][:, :], ALU.add).then_inc(o_add, 1)

        pool.sem_inc(o_add, CREDIT)
        run(pool, batch, batch)

    @block.scalar
    def _(act):
        def batch(b, par, tiles=TILES):
            first = isinstance(b, int) and b == 0
            for n in range(TILES):
                for p, back in pairs_before(n, ACT_PAIRS):
                    if (first and back) or not (tiles or back):
                        continue
                    dst, src = copy_pair(act, p, b - back, (par + back) % 2)
                    act.activation(dst, src, ACT.Copy).then_inc(t_act, 1)
                if n == OCOPY_AT and not first:
                    wait(act, pv_mm, CREDIT + b)
                    wait(act, o_mm, CREDIT + b - 1)
                    act.activation(o_t[:, :], ps_o[:, :], ACT.Copy).then_inc(o_copy, 1)
                if tiles:
                    wait(act, s_max, TILES * b + n + 1)
                    if n == 0:
                        wait(act, o_div, CREDIT + b - 1)
                    act.activation(s_ring[:, n % RING, :], s_ring[:, n % RING, :], ACT.Exp,
                                   bias=low[:, n:n + 1], scale=-1.0, accum_out=lsum[par][:, n:n + 1]).then_inc(p_done, 1)

        act.sem_inc(o_copy, CREDIT)
        run(act, batch, lambda b, par: batch(b, par, 0))

    @block.vector
    def _(dve):
        dve.wait_ge(adj_in, 16)
        for t in range(T):
            dve.tensor_scalar(mask[:, t, :].rearrange("p (u q) -> p u q", u=T),
                              a_nat[:, t, :].rearrange("p (q u) -> p u q", u=T),
                              0.0, NEG, ALU.is_equal, ALU.mult).then_inc(mask_done, 1)
        dve.wait_ge(mask_done, T)

        def batch(b, par, tiles=TILES):
            first = isinstance(b, int) and b == 0
            for n in range(TILES):
                for p, back in pairs_before(n, DVE_PAIRS):
                    if (first and back) or not (tiles or back):
                        continue
                    dst, src = copy_pair(dve, p, b - back, (par + back) % 2)
                    dve.tensor_copy(dst, src).then_inc(t_dve, 1)
                if tiles:
                    wait(dve, s_mm, CREDIT + TILES * b + n + 1)
                    wait(dve, t_mm, TILES * b + n - RING + 1)
                    settle(dve, waits_met)
                    dve.tensor_tensor_reduce(s_ring[:, n % RING, :], ps_s[S_BANK[n]][:, :], mask[:, n // HEADS, :],
                                             -SCALE, 3.0e38, ALU.add, ALU.min, low[:, n:n + 1]).then_inc(s_max, 1)
                if n == FIN_AT and not first:
                    c, cp = b - 1, 1 - par
                    wait(dve, p_done, TILES * b)
                    dve.reciprocal(lsum[cp][:, :], lsum[cp][:, :]).then_inc(rl_done, 1)
                    wait(dve, rl_done, b)
                    wait(dve, o_mm, CREDIT + b)
                    wait(dve, o_out[cp], CREDIT + parity_count(c, cp, 16) - 16)
                    dve.tensor_tensor(o_n[cp][:, :].rearrange("p (a e) -> p a e", e=HD),
                                      ps_n[:, :].rearrange("p (a e) -> p a e", e=HD),
                                      lsum[cp][:, :].rearrange("p (a o) -> p a o", o=1).to_broadcast([128, TILES, HD]),
                                      ALU.mult).then_inc(o_div, 1)

        dve.sem_inc(o_div, CREDIT)
        run(dve, batch, lambda b, par: batch(b, par, 0))

    @block.tensor
    def _(pe):
        def transposes(n, b):
            p = n // 2
            wait(pe, p_done, TILES * b + n + 1)
            if n % 2 == 0:
                s, value = copied(p - 2, b) if p >= 2 else copied(p - 2 + PAIRS, b - 1)
                if not (isinstance(b, int) and b == 0 and p < 2):
                    wait(pe, s, value)
            for j in range(T):
                mm = pe.transpose(ps_t[p % 2][:, n % 2, j * 128:(j + 1) * 128],
                                  s_ring[:, n % RING, j * 128:(j + 1) * 128], ident[:, :])
            mm.then_inc(t_mm, 1)

        def batch(b, par, tiles=TILES):
            first = isinstance(b, int) and b == 0
            c, cp = b - 1, 1 - par
            for n in range(TILES):
                it, h = divmod(n, HEADS)
                if tiles:
                    if n == 0:
                        wait(pe, qk_in[par], parity_count(b, par, 128))
                    wait(pe, s_max, TILES * b + n - S_BACK[n] + 1)
                    pe.matmul(ps_s[S_BANK[n]][:, :], q_st[par][:, h, it * 128:(it + 1) * 128],
                              k_st[par][:, h, :], start=True, stop=True).then_inc(s_mm, 1)
                if n >= LAG and tiles:
                    transposes(n - LAG, b)
                if n < LAG and not first:
                    transposes(TILES + n - LAG, c)
                for k in range(*PV_RANGE[n]) if not first else ():
                    j, hh = divmod(k, HEADS)
                    if k == 0:
                        for p in (ACT_PAIRS[-1], DVE_PAIRS[-1]):
                            wait(pe, *copied(p, c))
                        wait(pe, v_in[cp], parity_count(c, cp, 16))
                        wait(pe, o_div, CREDIT + c)
                    cols = slice(HD * hh, HD * (hh + 1))
                    mm = pe.matmul(ps_o[cols, :], v_sb[cp][:, j, cols], p_t[cp][:, hh, j, :],
                                   start=(j == 0), stop=(j == T - 1), tile_position=(0, HD * hh))
                    if k == HEADS * T - 1:
                        mm.then_inc(pv_mm, 1)
                if n == OT_AT and not first:
                    wait(pe, o_copy, CREDIT + b)
                    for t in range(T):
                        mm = pe.transpose(ps_n[:, t * 128:(t + 1) * 128], o_t[:, t * 128:(t + 1) * 128], ident[:, :])
                    mm.then_inc(o_mm, 1)

        pe.sem_inc(s_mm, CREDIT)
        pe.sem_inc(pv_mm, CREDIT)
        pe.sem_inc(o_mm, CREDIT)
        run(pe, batch, lambda b, par: batch(b, par, 0))


def graph_block(nc, x, adj, alpha, w, d, fcw, fcb, wqkv, out):
    x1_dram = nc.dram_tensor("x1_dram", [B, 128, T, D], F32, kind="Internal").ap()
    qk_dram = nc.dram_tensor("qk_dram", [B, 128, 4, N], F32, kind="Internal").ap()
    v_dram = nc.dram_tensor("v_dram", [B, 128, N], F32, kind="Internal").ap()
    with nc.sbuf_tensor("ident", [128, 128], F32) as ident:
        keep = {"ident": ident}
        with ExitStack() as kept:
            def sb(name, shape, dt=F32R):
                return kept.enter_context(nc.sbuf_tensor(name, shape, dt))
            keep["pH"] = [sb(f"pH{k}", [128, T, N]) for k in range(3)]
            keep["pL"] = [sb(f"pL{k}", [128, T, N]) for k in range(3)]
            keep["rH"], keep["rL"] = sb("rH", [128, 3, 3 * D]), sb("rL", [128, 3, 3 * D])
            keep["wH"], keep["wL"] = sb("wH", [128, 3 * D]), sb("wL", [128, 3 * D])
            keep["g"] = sb("g", [128, T, 3 * D], F32)
            ln = FirstNorm(sb, lambda name: kept.enter_context(nc.semaphore(name)))
            with ExitStack() as ctx:
                setup_block(nc, ctx, x, adj, alpha, w, d, fcw, fcb, wqkv, keep, ln)
            with ExitStack() as ctx:
                ode_block(nc, ctx, x, x1_dram, qk_dram, v_dram, keep, ln)
        with ExitStack() as ctx:
            attention_block(nc, ctx, adj, x1_dram, qk_dram, v_dram, out, keep)


_INS = ["x", "adj", "L0_gnn_alpha_train", "L0_gnn_w", "L0_gnn_d", "L0_gnn_fc_in_w", "L0_gnn_fc_in_b", "L1_gnn_W"]


def kernel(**inputs):
    import numpy as np
    import concourse.bacc as bacc
    from concourse.bass_utils import run_bass_kernel_spmd

    nc = bacc.Bacc("TRN2", target_bir_lowering=False, num_devices=1)
    arrays, args = {}, []
    for name in _INS:
        a = np.ascontiguousarray(inputs[name])
        arrays[f"in_{name}"] = a
        args.append(nc.dram_tensor(f"in_{name}", a.shape, mybir.dt.from_np(a.dtype), kind="ExternalInput").ap())
    args.append(nc.dram_tensor("out_x", (B, N, D), F32, kind="ExternalOutput").ap())
    graph_block(nc, *args)
    r = run_bass_kernel_spmd(nc, [arrays], core_ids=[0])
    return r.results[0]["out_x"]
```

```python
from collections import namedtuple
from contextlib import ExitStack

import concourse.bass as bass
from concourse import mybir

F32 = mybir.dt.float32
F32R = mybir.dt.float32r
ALU = mybir.AluOpType
ACT = mybir.ActivationFunctionType

B, N, D = 16, 512, 128
HEADS = 4
HD = D // HEADS
T = N // 128
GB = 4
NG = B // GB
STEPS = 8
DT = 1.0 / STEPS
NC = STEPS + 1
EPS = 1e-5
NEG = -1e30
SCALE = float(HD) ** -0.5
CW = D + 1
CREDIT = 1
WARM_START, WARM_NORM, WARM_END = 20, 48, 16
LOOP_BATCHES = 2


def wait(eng, sem, value):
    if isinstance(value, int) and value <= 0:
        return
    eng.wait_ge(sem, value)


def nothing(*_):
    pass


Steps = namedtuple("Steps", "u v z y back tail", defaults=[nothing] * 6)


def settle(eng, waits_met):
    eng.sem_inc(waits_met, 1)


def batch_of(ap, b):
    return ap[b:b + 1] if isinstance(b, int) else ap[bass.ds(b, 1)]


def keep_warm(pe, bank, ident, count):
    for _ in range(count):
        pe.transpose(bank[:, 0:128], ident[:, :], ident[:, :])


def split3(eng, psum, pairs, first=True, last=True):
    mm = None
    for n, ((lh, ll), (rh, rl)) in enumerate(pairs):
        eng.matmul(psum, lh, rh, start=(first and n == 0), stop=False)
        eng.matmul(psum, lh, rl, start=False, stop=False)
        mm = eng.matmul(psum, ll, rh, start=False, stop=(last and n == len(pairs) - 1))
    return mm


class Norm:

    def __init__(self, sb, sem, name, eps):
        self.eps = eps
        self.stat = sb(name + "_stat", [128, T, 6], F32)
        self.mv = sb(name + "_mv", [128, T, 2], F32)
        self.std = sb(name + "_std", [128, T], F32)
        self.st_done, self.var_done, self.std_done, self.rs_done, self.norm_done = (
            sem(f"{name}_{what}") for what in ("st_done", "var_done", "std_done", "rs_done", "norm_done"))


def norm_stats(dve, nm, n, src, tiles):
    for t in tiles:
        ins = dve.bn_stats(nm.stat[:, t, :], src(t))
        if t == T - 1:
            ins.then_inc(nm.st_done, 1)


def norm_var(dve, nm, n):
    wait(dve, nm.st_done, n + 1)
    settle(dve, nm.waits_met)
    for t in range(T):
        last = dve.bn_aggr(nm.mv[:, t, :], nm.stat[:, t, :])
    last.then_inc(nm.var_done, 1)


def norm_root(act, nm, n):
    wait(act, nm.var_done, n + 1)
    act.activation(nm.std[:, :], nm.mv[:, :, 1], ACT.Sqrt, bias=nm.eps[:, 0:1]).then_inc(nm.std_done, 1)


def norm_recip(dve, nm, n):
    wait(dve, nm.std_done, n + 1)
    dve.reciprocal(nm.std[:, :], nm.std[:, :]).then_inc(nm.rs_done, 1)
    wait(dve, nm.rs_done, n + 1)
    wait(dve, nm.var_done, n + 1)


def norm_scale(dve, nm, src, dst, tiles):
    for t in tiles:
        ins = dve.tensor_scalar(dst(t), src(t), nm.mv[:, t, 0:1], nm.std[:, t:t + 1], ALU.subtract, ALU.mult)
        if t == T - 1:
            ins.then_inc(nm.norm_done, 1)


class FirstNorm:

    def __init__(self, sb, sem):
        self.x_ln = [sb(f"x_ln{i}", [128, T, D], F32) for i in range(2)]
        self.u0 = sb("u0", [128, GB, T, D], F32)
        self.u0_h = sb("u0_h", [128, GB, T, D])
        self.u0_l = sb("u0_l", [128, GB, T, D])
        eps = sb("eps", [128, 1], F32)
        self.norm = Norm(sb, sem, "ln1", eps)
        self.waits_met = self.norm.waits_met = sem("waits_met")
        self.eps_done = sem("eps_done")
        self.xl_in = [sem(f"xl_in{i}") for i in range(2)]
        self.u0_done, self.u0h_done, self.u0l_done = sem("u0_done"), sem("u0h_done"), sem("u0l_done")
        self.u_mm = sem("u_mm")


def first_norm_load(eng, ln, x, g, b):
    wait(eng, ln.norm.norm_done, GB * g + b - 1)
    eng.dma_start(ln.x_ln[b % 2][:, :, :],
                  batch_of(x, GB * g + b).rearrange("o (p t) d -> p (o t) d", t=T)).then_inc(ln.xl_in[b % 2], 16)


def first_norm_dve(dve, ln, g, b, part):
    n = GB * g + b

    def src(t):
        return ln.x_ln[b % 2][:, t, :]

    if part == 0:
        wait(dve, ln.xl_in[b % 2], 16 * (2 * g + b // 2 + 1))
        norm_stats(dve, ln.norm, n, src, range(T))
    elif part == 1:
        norm_var(dve, ln.norm, n)
    elif part == 2:
        norm_recip(dve, ln.norm, n)
        wait(dve, ln.u_mm, 3 * (n - GB) + 3)
        wait(dve, ln.u0l_done, n - GB + 1)
        norm_scale(dve, ln.norm, src, lambda t: ln.u0[:, b, t, :], range(T // 2))
    else:
        norm_scale(dve, ln.norm, src, lambda t: ln.u0[:, b, t, :], range(T // 2, T))


def first_norm_act(act, ln, g, b):
    n = GB * g + b
    wait(act, ln.norm.norm_done, n + 1)
    act.activation(ln.u0[:, b, :, :], ln.u0[:, b, :, :], ACT.Relu).then_inc(ln.u0_done, 1)
    wait(act, ln.u0_done, n + 1)
    wait(act, ln.u_mm, 3 * (n - GB) + 3)
    act.activation(ln.u0_h[:, b, :, :], ln.u0[:, b, :, :], ACT.Copy).then_inc(ln.u0h_done, 1)


def first_norm_pool(pool, ln, g, b):
    n = GB * g + b
    wait(pool, ln.u0h_done, n + 1)
    wait(pool, ln.u_mm, 3 * (n - GB) + 3)
    pool.tensor_tensor(ln.u0_l[:, b, :, :], ln.u0[:, b, :, :], ln.u0_h[:, b, :, :].bitcast(F32),
                       ALU.subtract).then_inc(ln.u0l_done, 1)


def setup_block(nc, ctx, x, adj, alpha, w, d, fcw, fcb, wqkv, keep, ln):
    def sb(name, shape, dt=F32):
        return ctx.enter_context(nc.sbuf_tensor(name, shape, dt))

    def sem(name):
        return ctx.enter_context(nc.semaphore(name))

    a_nat = sb("a_nat", [128, T, N])
    alpha_sb = sb("alpha_sb", [128, T])
    s_col = sb("s_col", [128, T])
    table = sb("table", [128, 1])
    e_col = sb("e_col", [128, T])
    c_col = sb("c_col", [128, T])
    w_sb = sb("w_sb", [128, D])
    d_sb = sb("d_sb", [128, 1])
    d_dt = sb("d_dt", [128, 1])
    w_qkv = sb("w_qkv", [128, 3 * D])
    p_nat = sb("p_nat", [128, T, N])
    p_h = sb("p_h", [128, T, N], F32R)
    p_l = sb("p_l", [128, T, N], F32R)
    w_t = sb("w_t", [128, D])
    w_td = sb("w_td", [128, D])
    q_sb = sb("q_sb", [128, D])
    coef = [sb(f"coef{i}", [128, NC + 1, CW]) for i in range(2)]
    pick = sb("pick", [128, 2, 3], F32R)
    s_rows = sb("s_rows", [3, N])
    c_rows = sb("c_rows", [3, 3 * D])

    ps_p = [ctx.enter_context(nc.psum_tensor(f"ps_p{i}", [128, 512], F32)) for i in range(4)]
    ps_c = ctx.enter_context(nc.psum_tensor("ps_c", [128, 3, 512], F32))
    ps_w = ctx.enter_context(nc.psum_tensor("ps_w", [128, 512], F32))

    adj_in = [sem(f"adj_in{t}") for t in range(T)]
    alpha_in, w_in, f_in, q_in = (sem(n) for n in ("alpha_in", "w_in", "f_in", "q_in"))
    exp_done, col_done, ident_done, coef_zero = (sem(n) for n in ("exp_done", "col_done", "ident_done", "coef_zero"))
    p_done, ph_done, pl_done = (sem(n) for n in ("p_done", "ph_done", "pl_done"))
    pow_mm, pow_h, pow_l = (sem(n) for n in ("pow_mm", "pow_h", "pow_l"))
    w_mm, w_done, table_in = sem("w_mm"), sem("w_done"), sem("table_in")
    coef_mm, coef_done, coef_ready = sem("coef_mm"), sem("coef_done"), sem("coef_ready")
    r_mm, r_h, r_l = sem("r_mm"), sem("r_h"), sem("r_l")
    row_mm, row_done, g_mm, g_done = (sem(n) for n in ("row_mm", "row_done", "g_mm", "g_done"))
    qw_h, qw_l, pick_done = sem("qw_h"), sem("qw_l"), sem("pick_done")

    ident = keep["ident"]

    def bank_g(t):
        return ps_c[:, t, 0:3 * D] if t < 3 else ps_p[3][:, 0:3 * D]

    block = ctx.enter_context(nc.Block())

    @block.sync
    def _(sp):
        for t in range(T):
            sp.dma_start(a_nat[:, t:t + 1, :], adj.rearrange("(p t) m -> p t m", t=T)[:, t:t + 1, :]).then_inc(adj_in[t], 16)
        sp.wait_ge(coef_zero, 2)
        sp.dma_start(coef[0][:, 1, 0:D], fcw).then_inc(f_in, 16)
        sp.dma_start(coef[0][:, 1, D:CW], fcb.rearrange("(p o) -> p o", o=1)).then_inc(f_in, 16)
        for b in range(GB):
            first_norm_load(sp, ln, x, 0, b)
            if b == 1:
                sp.dma_start(w_qkv[:, :], wqkv).then_inc(q_in, 16)

    @block.gpsimd
    def _(pool):
        pool.memset(ln.norm.eps[:, :], EPS).then_inc(ln.eps_done, 1)
        pool.memset(ident[:, :], 0.0).then_inc(ident_done, 1)
        pool.wait_ge(ident_done, 1)
        pool.affine_select(out=ident[:, :], in_=ident[:, :], compare_op=ALU.not_equal, fill=1.0,
                           base=0, pattern=[[-1, 128]], channel_multiplier=1).then_inc(ident_done, 1)
        for c in coef:
            pool.memset(c[:, :, :], 0.0).then_inc(coef_zero, 1)
        pool.memset(pick[:, :, :].bitcast(F32), 0.0).then_inc(pick_done, 1)
        pool.wait_ge(pick_done, 1)
        for j in range(2):
            pool.memset(pick[:, j, j + 1:j + 2].bitcast(F32), 1.0).then_inc(pick_done, 1)
        for t in range(T):
            pool.wait_ge(ph_done, t + 1)
            pool.tensor_tensor(p_l[:, t, :], p_nat[:, t, :], p_h[:, t, :].bitcast(F32), ALU.subtract).then_inc(pl_done, 1)
        for b in range(GB):
            first_norm_pool(pool, ln, 0, b)

    @block.scalar
    def _(act):
        act.dma_start(alpha_sb[:, :], alpha.rearrange("(p t) -> p t", t=T)).then_inc(alpha_in, 16)
        act.wait_ge(ln.eps_done, 1)
        act.activation(table[:, :], ln.norm.eps[:, :], ACT.Exp).then_inc(table_in, 1)
        act.dma_start(w_sb[:, :], w).then_inc(w_in, 16)
        act.dma_start(d_sb[:, :], d.rearrange("(p o) -> p o", o=1)).then_inc(w_in, 16)
        act.wait_ge(alpha_in, 16)
        act.activation(e_col[:, :], alpha_sb[:, :], ACT.Exp, scale=-1.0).then_inc(exp_done, 1)
        for t in range(T):
            act.wait_ge(p_done, t + 1)
            act.activation(p_h[:, t, :], p_nat[:, t, :], ACT.Copy).then_inc(ph_done, 1)
        for k in range(3):
            if k == 1:
                act.wait_ge(q_in, 16)
                act.activation(keep["wH"][:, :], w_qkv[:, :], ACT.Copy).then_inc(qw_h, 1)
            for m in range(T):
                act.wait_ge(pow_mm, k * T + m + 1)
                act.activation(keep["pH"][k][:, m, :], ps_p[m][:, :], ACT.Copy).then_inc(pow_h, 1)
                n = (k - 1) * T + m
                if n == 0:
                    act.wait_ge(ln.eps_done, 1)
                if k >= 1 and n % 2 == 0:
                    norm_root(act, ln.norm, n // 2)
                elif k >= 1:
                    first_norm_act(act, ln, 0, n // 2)
        act.wait_ge(row_mm, 2)
        act.activation(c_rows[:, :], ps_p[3][0:3, 0:3 * D], ACT.Copy).then_inc(row_done, 1)
        for j in range(3):
            act.wait_ge(r_mm, j + 1)
            act.activation(keep["rH"][:, j, :], ps_p[j][:, 0:3 * D], ACT.Copy).then_inc(r_h, 1)
        for t in range(T):
            act.wait_ge(g_mm, t + 1)
            act.activation(keep["g"][:, t, :], bank_g(t), ACT.Copy).then_inc(g_done, 1)

    @block.vector
    def _(dve):
        n_col = 0

        def col(ins):
            nonlocal n_col
            n_col += 1
            ins.then_inc(col_done, 1)
            dve.wait_ge(col_done, n_col)

        dve.wait_ge(exp_done, 1)
        col(dve.tensor_scalar(e_col[:, :], e_col[:, :], 1.0, None, ALU.add))
        col(dve.reciprocal(s_col[:, :], e_col[:, :]))
        col(dve.tensor_scalar(s_col[:, :], s_col[:, :], 0.5 * DT, None, ALU.mult))
        col(dve.tensor_scalar(c_col[:, :], s_col[:, :], -1.0, 1.0 - DT, ALU.mult, ALU.add))
        dve.wait_ge(ident_done, 2)
        for t in range(T):
            dve.wait_ge(adj_in[t], 16)
            dst = p_nat[:, t, :].rearrange("p (u q) -> p u q", u=T)
            src = a_nat[:, t, :].rearrange("p (q u) -> p u q", u=T)
            col(dve.tensor_scalar(dst, src, s_col[:, t:t + 1], None, ALU.mult))
            diag = p_nat[:, t, t * 128:(t + 1) * 128]
            dve.scalar_tensor_tensor(out=diag, in0=ident[:, :], scalar=c_col[:, t:t + 1], in1=diag,
                                     op0=ALU.mult, op1=ALU.add).then_inc(p_done, 1)
        dve.wait_ge(w_in, 32)
        col(dve.tensor_scalar(d_dt[:, :], d_sb[:, :], 0.0, 1.0, ALU.max, ALU.min))
        col(dve.tensor_scalar(d_dt[:, :], d_dt[:, :], DT, None, ALU.mult))
        dve.wait_ge(w_mm, 1)
        dve.tensor_copy(w_t[:, :], ps_w[:, 0:D])
        dve.tensor_scalar(w_td[:, :], ps_w[:, 0:D], d_dt[:, 0:1], None, ALU.mult).then_inc(w_done, 1)
        dve.wait_ge(w_mm, 2)
        dve.tensor_copy(q_sb[:, :], ps_w[:, 0:D]).then_inc(w_done, 1)
        dve.wait_ge(coef_zero, 2)
        for c in coef:
            dve.tensor_scalar(c[:, 0, 0:D], ident[:, :], DT, None, ALU.mult).then_inc(coef_ready, 1)
        dve.wait_ge(coef_ready, 2)
        dve.wait_ge(f_in, 32)

        def low(k, m):
            dve.wait_ge(pow_h, k * T + m + 1)
            dve.tensor_tensor(keep["pL"][k][:, m, :], ps_p[m][:, :], keep["pH"][k][:, m, :].bitcast(F32),
                              ALU.subtract).then_inc(pow_l, 1)

        def step(n):
            old, new = coef[n % 2], coef[(n + 1) % 2]
            if n:
                dve.wait_ge(coef_done, n)
            dve.tensor_copy(new[:, n + 2, :], old[:, n + 1, :])
            dve.wait_ge(coef_mm, n + 1)
            for s in range(1, n + 2, 3):
                k = min(3, n + 2 - s)
                last = dve.tensor_tensor(new[:, s:s + k, :],
                                         ps_c[:, (s - 1) // 3, 0:k * CW].rearrange("p (k c) -> p k c", c=CW),
                                         old[:, s - 1:s - 1 + k, :], ALU.add)
            last.then_inc(coef_done, 1)

        for m in range(T):
            low(0, m)
        for n in range(STEPS):
            step(n)
            for part in (0, 1) if n % 2 == 0 else (2,):
                first_norm_dve(dve, ln, 0, n // 2, part)
            low(1 + n // T, n % T)
            if n % 2:
                first_norm_dve(dve, ln, 0, n // 2, 3)
        dve.wait_ge(qw_h, 1)
        dve.tensor_tensor(keep["wL"][:, :], w_qkv[:, :], keep["wH"][:, :].bitcast(F32),
                          ALU.subtract).then_inc(qw_l, 1)
        dve.wait_ge(row_mm, 1)
        dve.tensor_scalar(s_rows[:, :], ps_w[0:3, :], ident[0:3, 0:1], None, ALU.add).then_inc(row_done, 1)
        for j in range(3):
            dve.wait_ge(r_h, j + 1)
            dve.tensor_tensor(keep["rL"][:, j, :], ps_p[j][:, 0:3 * D], keep["rH"][:, j, :].bitcast(F32),
                              ALU.subtract).then_inc(r_l, 1)

    @block.tensor
    def _(pe):
        pe.wait_ge(ident_done, 2)
        keep_warm(pe, ps_p[0], ident, WARM_START)
        pe.wait_ge(w_in, 32)
        pe.transpose(ps_w[:, 0:D], w_sb[:, :], ident[:, :]).then_inc(w_mm, 1)
        for t in range(T):
            pe.wait_ge(p_done, t + 1)
            for m in range(T):
                tr = pe.transpose(ps_p[m][:, t * 128:(t + 1) * 128], p_nat[:, t, m * 128:(m + 1) * 128], ident[:, :])
                if t == T - 1:
                    tr.then_inc(pow_mm, 1)
        pe.wait_ge(w_done, 1)
        pe.matmul(ps_w[:, 0:D], w_td[:, :], w_t[:, :], start=True, stop=True).then_inc(w_mm, 1)
        pe.wait_ge(w_done, 2)
        pe.wait_ge(f_in, 32)
        pe.wait_ge(coef_zero, 2)
        pe.wait_ge(coef_ready, 2)

        def power(k, m):
            pe.wait_ge(pow_l, (k - 1) * T + m + 1)
            rows = slice(m * 128, (m + 1) * 128)
            high, low = keep["pH"][k - 1], keep["pL"][k - 1]
            pe.wait_ge(ph_done, T)
            for c in range(T):
                pe.wait_ge(pow_h, (k - 1) * T + c + 1)
                pe.matmul(ps_p[m][:, :], p_h[:, c, rows], high[:, c, :], start=(c == 0), stop=False)
            for c in range(T):
                pe.wait_ge(pl_done, c + 1)
                pe.matmul(ps_p[m][:, :], p_l[:, c, rows], high[:, c, :], start=False, stop=False)
            for c in range(T):
                pe.wait_ge(pow_l, (k - 1) * T + c + 1)
                mm = pe.matmul(ps_p[m][:, :], p_h[:, c, rows], low[:, c, :], start=False, stop=(c == T - 1))
            mm.then_inc(pow_mm, 1)

        for n in range(STEPS):
            if n:
                pe.wait_ge(coef_done, n)
            for s in range(1, n + 2, 3):
                k = min(3, n + 2 - s)
                mm = pe.matmul(ps_c[:, (s - 1) // 3, 0:k * CW], q_sb[:, :],
                               coef[n % 2][:, s:s + k, :].rearrange("p k c -> p (k c)"), start=True, stop=True)
            mm.then_inc(coef_mm, 1)
            power(1 + n // T, n % T)
        pe.wait_ge(pick_done, 3)
        for j in range(2):
            for m in range(T):
                for part in ("pH", "pL"):
                    mm = pe.matmul(ps_w[0:3, :], pick[:, j, :], keep[part][j][:, m, :],
                                   start=(j == 0 and m == 0 and part == "pH"),
                                   stop=(j == 1 and m == T - 1 and part == "pL"))
        mm.then_inc(row_mm, 1)
        fin = coef[STEPS % 2]
        pe.wait_ge(coef_done, STEPS)
        pe.wait_ge(pow_l, 3 * T)
        for i in range(3):
            tr = pe.transpose(ps_p[3][0:3, i * D:(i + 1) * D], fin[:, 1 + 3 * i:4 + 3 * i, D], ident[:, :])
        tr.then_inc(row_mm, 1)
        for j in range(3):
            for i in range(3):
                tr = pe.transpose(ps_p[j][:, i * D:(i + 1) * D], fin[:, 1 + 3 * i + j, 0:D], ident[:, :])
            tr.then_inc(r_mm, 1)
        pe.wait_ge(row_done, 2)
        for t in range(T):
            pe.matmul(bank_g(t), s_rows[:, t * 128:(t + 1) * 128], c_rows[:, :],
                      start=True, stop=True).then_inc(g_mm, 1)


def ode_block(nc, ctx, x, adj, x1_dram, qk_dram, v_dram, keep, ln):
    def sb(name, shape, dt=F32):
        return ctx.enter_context(nc.sbuf_tensor(name, shape, dt))

    def sem(name):
        return ctx.enter_context(nc.semaphore(name))

    def bank(name):
        return ctx.enter_context(nc.psum_tensor(name, [128, 512], F32))

    x_res = sb("x_res", [128, T, D])
    ut_h = [sb(f"ut_h{i}", [128, 3, N], F32R) for i in range(2)]
    ut_l = [sb(f"ut_l{i}", [128, 3, N], F32R) for i in range(2)]
    v = sb("v", [128, T, GB, 3 * D])
    v2_h = sb("v2_h", [128, T, GB, D], F32R)
    v2_l = sb("v2_l", [128, T, GB, D], F32R)
    z_h = sb("z_h", [128, T, GB, D], F32R)
    z_l = sb("z_l", [128, T, GB, D], F32R)
    h2 = sb("h2", [128, GB, T, D])
    ht_h = [sb(f"ht_h{i}", [128, N], F32R) for i in range(2)]
    ht_l = [sb(f"ht_l{i}", [128, N], F32R) for i in range(2)]
    qk = [sb(f"qk{i}", [128, 2, N], F32R) for i in range(2)]
    vt = [sb(f"vt{i}", [128, N]) for i in range(2)]
    v_nat = sb("v_nat", [128, N])
    stat_all = sb("stat_all", [128, GB * T, 6])
    mv_all = sb("mv_all", [128, GB * T, 2])
    std_all = sb("std_all", [128, GB * T])
    exp_out = sb("exp_out", [128, 1])
    ln2n = Norm(sb, sem, "ln2", ln.norm.eps)

    ps_u = [bank(f"ps_u{i}") for i in range(2)]
    ps_v = [bank(f"ps_v{i}") for i in range(2)]
    ps_z = [bank(f"ps_z{i}") for i in range(2)]
    ps_k = [bank(f"ps_k{i}") for i in range(2)]

    ident = keep["ident"]
    waits_met = ln.waits_met
    ln2n.waits_met = waits_met
    u0, u0_h, u0_l, u0_done, u0l_done = ln.u0, ln.u0_h, ln.u0_l, ln.u0_done, ln.u0l_done
    xr_in = sem("xr_in")
    u_mm, uh_done, ul_done = ln.u_mm, sem("uh_done"), sem("ul_done")
    v_mm, v_add, v2h_done, v2l_done, xv_done = (sem(n) for n in ("v_mm", "v_add", "v2h_done", "v2l_done", "xv_done"))
    z_mm, z_add, zh_done, zl_done = (sem(n) for n in ("z_mm", "z_add", "zh_done", "zl_done"))
    y_mm, x1_add, x1_out = sem("y_mm"), sem("x1_add"), sem("x1_out")
    h2_done = sem("h2_done")
    k_mm, kh_done, kl_done, vt_done, vn_done = (sem(n) for n in ("k_mm", "kh_done", "kl_done", "vt_done", "vn_done"))
    qk_out = [sem(f"qk_out{i}") for i in range(2)]
    qk1_out = [sem(f"qk1_out{i}") for i in range(2)]
    v_out = sem("v_out")
    tail_st, tail_var, tail_std, tail_rs, tail_norm = (
        sem(n) for n in ("tail_st", "tail_var", "tail_std", "tail_rs", "tail_norm"))
    exp_ready = sem("exp_ready")
    tail_out = keep["tail_out"]

    BACK = [("t", 0), ("t", 1), ("q", 0), ("k", 0), ("vt", 0), ("q", 1), ("k", 1), ("vt", 1), ("v", 0), ("v", 1)]
    NB = len(BACK)
    BACK_BANKS = [*ps_k, *ps_u]
    NK = len(BACK_BANKS)

    def u_bank(b, k):
        return ps_v[0] if (b, k) == (0, 2) else ps_u[(3 * b + k) % 2]

    def has_prev(g):
        return not (isinstance(g, int) and g == 0)

    def qk_parts(kind, pair, c):
        which = 0 if kind == "q" else 1
        if c == 0:
            return [qk[which][:, part, :] for part in range(2)]
        return [part[:, 2 + which, :, :].rearrange("p b d -> p (b d)") for part in ((z_h, z_l), (v2_h, v2_l))[pair]]

    SPLIT = [i for i, (kind, _) in enumerate(BACK) if kind in "tqk"]
    VT = [i for i, (kind, _) in enumerate(BACK) if kind == "vt"]
    VN = [i for i, (kind, _) in enumerate(BACK) if kind == "v"]

    def freed(i, pair):
        if i in SPLIT:
            return kl_done, len(SPLIT) * pair + SPLIT.index(i) + 1
        if i in VT:
            return vt_done, len(VT) * pair + VT.index(i) + 1
        return vn_done, len(VN) * pair + VN.index(i) + 1

    TAIL = [("t", 0), ("t", 1), ("q", 0), ("k", 0), ("vt", 0), ("t", 2), ("q", 1), ("k", 1), ("vt", 1), ("t", 3),
            ("v", 0), ("q", 2), ("k", 2), ("vt", 2), ("v", 1), ("q", 3), ("k", 3), ("vt", 3), ("v", 2), ("v", 3)]
    TAIL_BANKS = [*ps_k, *ps_u, *ps_v, *ps_z]
    LAST = NG - 1

    def tail_count(i):
        kinds = {"t": "tqk", "q": "tqk", "k": "tqk", "vt": ("vt",), "v": ("v",)}[TAIL[i][0]]
        nth = sum(kind in kinds for kind, _ in TAIL[:i + 1])
        each = sum(kind in kinds for kind, _ in TAIL)
        return {"t": kl_done, "q": kl_done, "k": kl_done, "vt": vt_done, "v": vn_done}[TAIL[i][0]], each * LAST + nth

    def tail_qk(kind, c):
        high, low = (v2_h, v2_l) if kind == "q" else (z_h, z_l)
        return [part[:, c, :, :].rearrange("p b d -> p (b d)") for part in (high, low)]

    def tail_v(c):
        return h2[:, c, :, :].rearrange("p t d -> p (t d)")

    def group(g, steps, prev=True, following=True):
        def back(pair, lo, hi):
            if prev:
                steps.back(g - 1, pair, lo, hi)
        steps.u(g, 0, prev)
        for b in range(1, GB):
            steps.u(g, b, prev)
            steps.v(g, b - 1, following)
        back(0, 0, 2)
        steps.v(g, GB - 1, following)
        back(0, 2, 8)
        for t in range(T):
            steps.z(g, t)
            if t < 2:
                back(0, 8 + t, 9 + t)
            if t == 2:
                back(1, 0, 2)
        back(1, 2, 8)
        for t in range(T):
            steps.y(g, t)
            if t < 2:
                back(1, 8 + t, 9 + t)

    def run(eng, steps):
        group(0, steps, prev=False)
        with eng.Fori(1, NG - 1) as g:
            group(g, steps)
        group(NG - 1, steps, following=False)
        steps.tail()

    block = ctx.enter_context(nc.Block())

    @block.sync
    def _(sp):
        def u_step(g, b, prev):
            if b == 0 and prev:
                store_x1(g - 1)

        def v_step(g, b, following):
            if following:
                first_norm_load(sp, ln, x, g + 1, b)
            wait(sp, xv_done, GB * g + b)
            sp.dma_start(x_res[:, :, :], batch_of(x, GB * g + b).rearrange("o (p t) d -> p (o t) d", t=T)).then_inc(xr_in, 16)

        def store_x1(g):
            wait(sp, x1_add, T * (g + 1))
            for c in range(GB):
                sp.dma_start(batch_of(x1_dram, GB * g + c).rearrange("o p t d -> p (o t) d"), v[:, :, c, 0:D]).then_inc(x1_out, 16)

        def tail():
            wait(sp, ln.u_mm, 3 * B)
            wait(sp, ln.u0l_done, B)
            sp.dma_start(ln.u0[:, :, :, :].rearrange("p b t d -> p b (t d)"), adj.rearrange("(p t) m -> p t m", t=T)).then_inc(keep["adj_in"], 16)
            for s, done in zip((*qk_out, *qk1_out), (16, 16, 32, 32)):
                wait(sp, s, CREDIT + done * 2 * LAST)
            load_qk(sp, qk_dram, keep, 0, 0)
            wait(sp, x1_add, T * NG)
            for c in range(GB):
                sp.dma_start(batch_of(x1_dram, GB * LAST + c).rearrange("o p t d -> p (o t) d"),
                             v[:, :, c, 0:D]).then_inc(tail_out, 16)
            for i, (kind, c) in enumerate(TAIL):
                b = GB * LAST + c
                if kind in ("q", "k"):
                    which = 0 if kind == "q" else 1
                    wait(sp, *tail_count(i))
                    for part, src in enumerate(tail_qk(kind, c)):
                        row = 2 * which + part
                        sp.dma_start(batch_of(qk_dram, b)[:, :, row:row + 1, :].rearrange("o p s n -> p (o s n)"),
                                     src.bitcast(F32)).then_inc(tail_out, 16)
                if kind == "v":
                    wait(sp, *tail_count(i))
                    sp.dma_start(batch_of(v_dram, b).rearrange("o p n -> p (o n)"), tail_v(c)).then_inc(tail_out, 16)

        def back(g, pair, lo, hi):
            for i, (kind, c) in list(enumerate(BACK))[lo:hi]:
                b = 2 * pair + c
                if kind in ("q", "k"):
                    which = 0 if kind == "q" else 1
                    wait(sp, kl_done, len(SPLIT) * (2 * g + pair) + SPLIT.index(i) + 1)
                    if c == 0:
                        dst = batch_of(qk_dram, GB * g + b)[:, :, 2 * which:2 * which + 2, :].rearrange("o p s n -> p (o s) n")
                        sp.dma_start(dst, qk[which][:, :, :].bitcast(F32)).then_inc(qk_out[which], 16)
                    else:
                        for part, src in enumerate(qk_parts(kind, pair, c)):
                            row = 2 * which + part
                            dst = batch_of(qk_dram, GB * g + b)[:, :, row:row + 1, :].rearrange("o p s n -> p (o s n)")
                            sp.dma_start(dst, src.bitcast(F32)).then_inc(qk1_out[which], 16)
                if kind == "v":
                    wait(sp, vn_done, 2 * (2 * g + pair) + c + 1)
                    sp.dma_start(batch_of(v_dram, GB * g + b).rearrange("o p n -> p (o n)"), v_nat[:, :]).then_inc(v_out, 16)

        for s in (*qk_out, *qk1_out, v_out):
            sp.sem_inc(s, CREDIT)
        run(sp, Steps(u=u_step, v=v_step, back=back, tail=tail))
        sp.wait_ge(x1_out, 16 * GB * LAST)
        sp.wait_ge(v_out, CREDIT + 16 * GB * LAST)

    @block.gpsimd
    def _(pool):
        def v_step(g, b, following):
            n = GB * g + b
            wait(pool, v2h_done, n + 1)
            wait(pool, z_mm, T * g)
            pool.tensor_tensor(v2_l[:, :, b, :], v[:, :, b, 2 * D:3 * D], v2_h[:, :, b, :].bitcast(F32),
                               ALU.subtract).then_inc(v2l_done, 1)
            wait(pool, xr_in, 16 * (n + 1))
            wait(pool, v_add, T * (n + 1))
            pool.tensor_tensor(v[:, :, b, 0:D], v[:, :, b, 0:D], x_res[:, :, :], ALU.add).then_inc(xv_done, 1)
            if following:
                first_norm_pool(pool, ln, g + 1, b)

        def z_step(g, t):
            wait(pool, zh_done, T * g + t + 1)
            wait(pool, y_mm, T * g)
            pool.tensor_tensor(z_l[:, t, :, :], v[:, t, :, D:2 * D], z_h[:, t, :, :].bitcast(F32),
                               ALU.subtract).then_inc(zl_done, 1)

        def tail():
            wait(pool, keep["adj_in"], 16)
            wait(pool, ln.u_mm, 3 * B)
            for t in range(T):
                pool.tensor_scalar(keep["pL"][1][:, t, :].rearrange("p (u q) -> p u q", u=T),
                                   ln.u0[:, t, :, :].rearrange("p t d -> p (t d)").rearrange("p (q u) -> p u q", u=T),
                                   0.0, NEG, ALU.is_equal, ALU.mult).then_inc(keep["mask_done"], 1)

        run(pool, Steps(v=v_step, z=z_step, tail=tail))

    @block.scalar
    def _(act):
        def u_step(g, b, prev):
            for k in range(3):
                n = 3 * (GB * g + b) + k
                wait(act, u_mm, n + 1)
                wait(act, v_mm, T * (GB * g + b - 1))
                act.activation(ut_h[b % 2][:, k, :], u_bank(b, k)[:, :], ACT.Copy).then_inc(uh_done, 1)
                if k == 1 and b and prev:
                    relu(g - 1, b - 1)
            if prev:
                norm_root(act, ln2n, GB * (g - 1) + b)

        def relu(g, b):
            n = GB * g + b
            wait(act, ln2n.norm_done, n + 1)
            act.activation(h2[:, b, :, :], h2[:, b, :, :], ACT.Relu).then_inc(h2_done, 1)

        def tail():
            def tail_relu(c):
                wait(act, tail_norm, c + 1)
                act.activation(h2[:, c, :, :], h2[:, c, :, :], ACT.Relu).then_inc(h2_done, 1)

            wait(act, y_mm, T * NG)
            for s in qk1_out:
                wait(act, s, CREDIT + 32 * 2 * LAST)
            wait(act, tail_var, 1)
            act.activation(std_all[:, :], mv_all[:, :, 1], ACT.Sqrt, bias=ln2n.eps[:, 0:1]).then_inc(tail_std, 1)
            act.activation(exp_out[:, :], ln2n.eps[:, 0:1], ACT.Exp).then_inc(exp_ready, 1)
            tail_relu(0)
            for i, (kind, c) in enumerate(TAIL):
                if kind == "t" and c + 1 < GB:
                    tail_relu(c + 1)
                wait(act, k_mm, 2 * NB * LAST + i + 1)
                src = TAIL_BANKS[i % len(TAIL_BANKS)][:, :]
                if kind == "t":
                    act.activation(ht_h[c % 2][:, :], src, ACT.Copy).then_inc(kh_done, 1)
                elif kind in ("q", "k"):
                    act.activation(tail_qk(kind, c)[0], src, ACT.Copy).then_inc(kh_done, 1)
                elif kind == "vt":
                    act.activation(vt[c % 2][:, :], src, ACT.Copy).then_inc(vt_done, 1)
                else:
                    act.activation(tail_v(c), src, ACT.Copy).then_inc(vn_done, 1)

        def v_step(g, b, following):
            n = GB * g + b
            if b == GB - 1 and has_prev(g):
                relu(g - 1, b)
            if following:
                if b:
                    first_norm_act(act, ln, g + 1, b - 1)
                norm_root(act, ln.norm, n + GB)
            wait(act, v_add, T * (n + 1))
            wait(act, z_mm, T * g)
            for s in qk1_out:
                wait(act, s, CREDIT + 32 * 2 * (g - 1))
            act.activation(v2_h[:, :, b, :], v[:, :, b, 2 * D:3 * D], ACT.Copy).then_inc(v2h_done, 1)

        def z_step(g, t):
            if t == 0 and (not isinstance(g, int) or g != LAST):
                first_norm_act(act, ln, g + 1, GB - 1)
            if t >= 2:
                wait(act, qk1_out[t - 2], CREDIT + 32 * (2 * g - 1))
            wait(act, z_add, T * g + t + 1)
            wait(act, y_mm, T * g)
            act.activation(z_h[:, t, :, :], v[:, t, :, D:2 * D], ACT.Copy).then_inc(zh_done, 1)

        def back(g, pair, lo, hi):
            pr = 2 * g + pair
            for i, (kind, c) in list(enumerate(BACK))[lo:hi]:
                wait(act, k_mm, NB * pr + i + 1)
                src = BACK_BANKS[i % NK][:, :]
                if kind == "t":
                    if pair:
                        wait(act, k_mm, NB * (pr - 1) + VT[c] + 1)
                    act.activation(ht_h[c][:, :], src, ACT.Copy).then_inc(kh_done, 1)
                elif kind in ("q", "k"):
                    if c == 0:
                        wait(act, qk_out[0 if kind == "q" else 1], CREDIT + 16 * pr)
                    act.activation(qk_parts(kind, pair, c)[0], src, ACT.Copy).then_inc(kh_done, 1)
                elif kind == "vt":
                    if pair:
                        wait(act, k_mm, NB * (pr - 1) + VN[c] + 1)
                    act.activation(vt[c][:, :], src, ACT.Copy).then_inc(vt_done, 1)
                else:
                    wait(act, v_out, CREDIT + 16 * (2 * pr + c))
                    act.activation(v_nat[:, :], src, ACT.Copy).then_inc(vn_done, 1)

        run(act, Steps(u=u_step, v=v_step, back=back, z=z_step, tail=tail))

    @block.vector
    def _(dve):
        def x1_rows(b):
            return lambda t: v[:, t, b, 0:D]

        def u_step(g, b, prev):
            for k in range(3):
                n = 3 * (GB * g + b) + k
                wait(dve, uh_done, n + 1)
                wait(dve, v_mm, T * (GB * g + b - 1))
                dve.tensor_tensor(ut_l[b % 2][:, k, :], u_bank(b, k)[:, :],
                                  ut_h[b % 2][:, k, :].bitcast(F32), ALU.subtract).then_inc(ul_done, 1)
                if k == 0 and b and prev:
                    scale_h2(g - 1, b - 1)
                if k == 1 and prev:
                    wait(dve, x1_add, T * g)
                    norm_stats(dve, ln2n, GB * (g - 1) + b, x1_rows(b), range(T))
                    norm_var(dve, ln2n, GB * (g - 1) + b)

        def scale_h2(g, b):
            norm_recip(dve, ln2n, GB * g + b)
            norm_scale(dve, ln2n, x1_rows(b), lambda t: h2[:, b, t, :], range(T))

        def tail_stats(t):
            wait(dve, x1_add, T * LAST + t + 1)
            for c in range(GB):
                ins = dve.bn_stats(stat_all[:, c * T + t, :], v[:, t, c, 0:D])
            ins.then_inc(tail_st, 1)

        def tail():
            def tail_scale(c):
                for t in range(T):
                    n = c * T + t
                    ins = dve.tensor_scalar(h2[:, c, t, :], v[:, t, c, 0:D], mv_all[:, n, 0:1], std_all[:, n:n + 1],
                                            ALU.subtract, ALU.mult)
                ins.then_inc(tail_norm, 1)

            tail_stats(T - 1)
            wait(dve, tail_st, T)
            for n in range(GB * T):
                ins = dve.bn_aggr(mv_all[:, n, :], stat_all[:, n, :])
            ins.then_inc(tail_var, 1)
            wait(dve, tail_std, 1)
            dve.reciprocal(std_all[:, :], std_all[:, :]).then_inc(tail_rs, 1)
            wait(dve, tail_rs, 1)
            wait(dve, k_mm, 2 * NB * LAST)
            tail_scale(0)
            for i, (kind, c) in enumerate(TAIL):
                if kind == "t" and c + 1 < GB:
                    tail_scale(c + 1)
                if kind in ("t", "q", "k"):
                    wait(dve, kh_done, tail_count(i)[1])
                    high, low = (ht_h[c % 2][:, :], ht_l[c % 2][:, :]) if kind == "t" else tail_qk(kind, c)
                    dve.tensor_tensor(low, TAIL_BANKS[i % len(TAIL_BANKS)][:, :], high.bitcast(F32),
                                      ALU.subtract).then_inc(kl_done, 1)

        def v_step(g, b, following):
            for t in range(T):
                n = T * (GB * g + b) + t
                wait(dve, v_mm, n + 1)
                if t == 0:
                    wait(dve, x1_out, 16 * GB * g)
                    wait(dve, ln2n.norm_done, GB * (g - 1) + b + 1)
                    wait(dve, zl_done, T * g)
                    wait(dve, v2l_done, GB * (g - 1) + b + 1)
                dve.tensor_tensor(v[:, t, b, :], ps_v[t % 2][:, 0:3 * D], keep["g"][:, t, :],
                                  ALU.add).then_inc(v_add, 1)
                if following:
                    first_norm_dve(dve, ln, g + 1, b, t)
            if b == GB - 2 and has_prev(g):
                scale_h2(g - 1, b + 1)

        def z_step(g, t):
            wait(dve, z_mm, T * g + t + 1)
            wait(dve, v_add, T * GB * (g + 1))
            dve.tensor_tensor(v[:, t, :, D:2 * D], ps_z[t % 2][:, :].rearrange("p (b d) -> p b d", b=GB),
                              v[:, t, :, D:2 * D], ALU.add).then_inc(z_add, 1)

        def y_step(g, t):
            wait(dve, y_mm, T * g + t + 1)
            wait(dve, xv_done, GB * (g + 1))
            dve.tensor_tensor(v[:, t, :, 0:D], ps_z[t % 2][:, :].rearrange("p (b d) -> p b d", b=GB),
                              v[:, t, :, 0:D], ALU.add).then_inc(x1_add, 1)
            if isinstance(g, int) and g == LAST and t:
                tail_stats(t - 1)

        def back(g, pair, lo, hi):
            pr = 2 * g + pair
            for i, (kind, c) in list(enumerate(BACK))[lo:hi]:
                if i not in SPLIT:
                    continue
                wait(dve, kh_done, len(SPLIT) * pr + SPLIT.index(i) + 1)
                src = BACK_BANKS[i % NK][:, :]
                if kind == "t":
                    if pair:
                        wait(dve, k_mm, NB * (pr - 1) + VT[c] + 1)
                    dst, high = ht_l[c][:, :], ht_h[c][:, :]
                else:
                    if c == 0:
                        wait(dve, qk_out[0 if kind == "q" else 1], CREDIT + 16 * pr)
                    high, dst = qk_parts(kind, pair, c)
                dve.tensor_tensor(dst, src, high.bitcast(F32), ALU.subtract).then_inc(kl_done, 1)

        run(dve, Steps(u=u_step, v=v_step, back=back, z=z_step, y=y_step, tail=tail))

    @block.tensor
    def _(pe):
        def u_step(g, b, prev):
            nb = GB * g + b
            for k in range(3):
                n = 3 * nb + k
                ps = u_bank(b, k)
                if (b, k) == (0, 2):
                    wait(pe, v_add, T * nb)
                else:
                    wait(pe, ul_done, n - 2 if (b, k) == (1, 1) else n - 1)
                if k == 0:
                    wait(pe, u0_done, nb + 1)
                    for t in range(T):
                        mm = pe.transpose(ps[:, t * 128:(t + 1) * 128], u0[:, b, t, :], ident[:, :])
                else:
                    wait(pe, u0l_done, nb + 1)
                    mm = split3(pe, ps[:, :], [((u0_h[:, b, m, :], u0_l[:, b, m, :]),
                                                (keep["pH"][k - 1][:, m, :], keep["pL"][k - 1][:, m, :]))
                                               for m in range(T)])
                mm.then_inc(u_mm, 1)

        def v_step(g, b, following):
            nb = GB * g + b
            wait(pe, ul_done, 3 * nb + 3)
            for t in range(T):
                wait(pe, v_add, T * nb + t - 1)
                rows = slice(t * 128, (t + 1) * 128)
                split3(pe, ps_v[t % 2][:, 0:3 * D], [((ut_h[b % 2][:, k, rows], ut_l[b % 2][:, k, rows]),
                                                     (keep["rH"][:, k, :], keep["rL"][:, k, :]))
                                                    for k in range(3)]).then_inc(v_mm, 1)

        def cube(g, t, src_h, src_l, high_done, low_done):
            rows = slice(t * 128, (t + 1) * 128)
            high, low = (keep[part][2] for part in ("pH", "pL"))
            for m in range(T):
                src = src_h[:, m, :, :].rearrange("p b d -> p (b d)")
                if t == 0:
                    high_done(m)
                pe.matmul(ps_z[t % 2][:, :], high[:, m, rows], src, start=(m == 0), stop=False)
                pe.matmul(ps_z[t % 2][:, :], low[:, m, rows], src, start=False, stop=False)
            for m in range(T):
                if t == 0:
                    low_done(m)
                mm = pe.matmul(ps_z[t % 2][:, :], high[:, m, rows], src_l[:, m, :, :].rearrange("p b d -> p (b d)"),
                               start=False, stop=(m == T - 1))
            return mm

        def z_step(g, t):
            if t < 2:
                wait(pe, x1_add, T * g - 2 + t + 1)
            else:
                wait(pe, z_add, T * g + t - 1)
            cube(g, t, v2_h, v2_l, lambda m: wait(pe, v2h_done, GB * (g + 1)),
                 lambda m: wait(pe, v2l_done, GB * (g + 1))).then_inc(z_mm, 1)

        def y_step(g, t):
            if t < 2:
                wait(pe, z_add, T * g + 2 + t + 1)
            else:
                wait(pe, x1_add, T * g + t - 1)
            cube(g, t, z_h, z_l, lambda m: wait(pe, zh_done, T * g + m + 1),
                 lambda m: wait(pe, zl_done, T * g + m + 1)).then_inc(y_mm, 1)

        def back(g, pair, lo, hi):
            pr = 2 * g + pair
            for i, (kind, c) in list(enumerate(BACK))[lo:hi]:
                ps = BACK_BANKS[i % NK]
                if i >= NK:
                    wait(pe, *freed(i - NK, pr))
                elif pair:
                    wait(pe, *freed(max(j for j in range(NB) if j % NK == i), pr - 1))
                if kind == "t":
                    b = 2 * pair + c
                    wait(pe, h2_done, GB * g + b + 1)
                    for t in range(T):
                        mm = pe.transpose(ps[:, t * 128:(t + 1) * 128], h2[:, b, t, :], ident[:, :])
                elif kind == "v":
                    wait(pe, vt_done, 2 * pr + c + 1)
                    for t in range(T):
                        mm = pe.transpose(ps[:, t * 128:(t + 1) * 128], vt[c][:, t * 128:(t + 1) * 128], ident[:, :])
                else:
                    wait(pe, kl_done, len(SPLIT) * pr + c + 1)
                    at = {"q": 0, "k": D, "vt": 2 * D}[kind]
                    mm = split3(pe, ps[:, :], [((keep["wH"][:, at:at + D], keep["wL"][:, at:at + D]),
                                                (ht_h[c][:, :], ht_l[c][:, :]))])
                mm.then_inc(k_mm, 1)

        def tail():
            keep_warm(pe, ps_v[0], ident, WARM_NORM)
            for i, (kind, c) in enumerate(TAIL):
                ps = TAIL_BANKS[i % len(TAIL_BANKS)]
                if i < NK:
                    wait(pe, *freed(max(j for j in range(NB) if j % NK == i), 2 * LAST - 1))
                elif i < 6:
                    wait(pe, v_add, T * B)
                elif i < 8:
                    wait(pe, x1_add, T * NG)
                else:
                    wait(pe, *tail_count(i - len(TAIL_BANKS)))
                if kind == "t":
                    wait(pe, h2_done, GB * LAST + c + 1)
                    for t in range(T):
                        mm = pe.transpose(ps[:, t * 128:(t + 1) * 128], h2[:, c, t, :], ident[:, :])
                elif kind == "v":
                    wait(pe, *tail_count(TAIL.index(("vt", c))))
                    for t in range(T):
                        mm = pe.transpose(ps[:, t * 128:(t + 1) * 128], vt[c % 2][:, t * 128:(t + 1) * 128], ident[:, :])
                else:
                    wait(pe, *tail_count(TAIL.index(("t", c))))
                    at = {"q": 0, "k": D, "vt": 2 * D}[kind]
                    mm = split3(pe, ps[:, :], [((keep["wH"][:, at:at + D], keep["wL"][:, at:at + D]),
                                                (ht_h[c % 2][:, :], ht_l[c % 2][:, :]))])
                mm.then_inc(k_mm, 1)

            wait(pe, *tail_count(TAIL_BANKS.index(ps_v[0]) + len(TAIL_BANKS)))
            keep_warm(pe, ps_v[0], ident, WARM_END)

        run(pe, Steps(u=u_step, v=v_step, back=back, z=z_step, y=y_step, tail=tail))


def load_qk(sp, qk_dram, keep, b, par):
    src = batch_of(qk_dram, b)
    for slot in range(4):
        for st, part in ((keep["q_st"], slot // 2), (keep["k_st"], 2 + slot % 2)):
            sp.dma_start(st[par][HD * slot:HD * (slot + 1), :, :].bitcast(F32),
                         src[:, :, part:part + 1, :].rearrange("o (h e) s n -> e (o s h) n", e=HD)).then_inc(keep["qk_in"][par], 16)


def attention_block(nc, ctx, x1_dram, qk_dram, v_dram, out, keep):
    def sb(name, shape, dt=F32):
        return ctx.enter_context(nc.sbuf_tensor(name, shape, dt))

    def sem(name):
        return ctx.enter_context(nc.semaphore(name))

    TILES = T * HEADS
    PAIRS = TILES // 2
    RING = 8
    LAG = 4
    ACT_PAIRS = [1, 2, 5, 7]
    DVE_PAIRS = [p for p in range(PAIRS) if p not in ACT_PAIRS]
    COPY_BEFORE = [7, 7, 8, 12, 14, 15, 18, 18]
    PV_AT = {5: 1, 6: 4, 7: 2, 11: 4, 13: 5}
    OCOPY_AT, OT_AT, FIN_AT = 13, 15, 15
    assert sum(PV_AT.values()) == HEADS * T
    PV_RANGE = [(sum(PV_AT.get(i, 0) for i in range(n)), sum(PV_AT.get(i, 0) for i in range(n + 1))) for n in range(TILES)]
    S_BANKS = 3
    S_BANK = [n % S_BANKS for n in range(TILES - 1)] + [1]
    S_BACK = [next(k for k in range(1, TILES) if S_BANK[n - k] == S_BANK[n]) for n in range(TILES)]

    mask, q_st, k_st = keep["pL"][1][:, :, :].bitcast(F32), keep["q_st"], keep["k_st"]
    s_ring = sb("s_ring", [128, RING, N])
    p_t = [sb("p_t0", [128, HEADS, T, N])]
    low = sb("low", [128, TILES])
    lsum = [sb(f"lsum{i}", [128, TILES]) for i in range(2)]
    p_t += [sb("p_t1", [128, HEADS, T, N])]
    o_t = sb("o_t", [128, N])
    o_n = [sb(f"o_n{i}", [128, T * D]) for i in range(2)]
    v_sb = [sb(f"v_sb{i}", [128, T, D]) for i in range(2)]
    x1 = [sb(f"x1_{i}", [128, T * D]) for i in range(2)]

    ps_s = [ctx.enter_context(nc.psum_tensor(f"ps_s{i}", [128, N], F32)) for i in range(S_BANKS)]
    ps_t = [ctx.enter_context(nc.psum_tensor(f"ps_t{i}", [128, 2, N], F32)) for i in range(2)]
    ps_o = ctx.enter_context(nc.psum_tensor("ps_o", [128, N], F32))
    ps_n = ps_o

    ident = keep["ident"]
    waits_met = sem("waits_met2")
    qk_in, mask_done, tail_out = keep["qk_in"], keep["mask_done"], keep["tail_out"]
    TAIL_STORED = 16 * GB * (1 + 4 + 1)
    v_in = [sem(f"v_in{i}") for i in range(2)]
    x_in = [sem(f"x_in{i}") for i in range(2)]
    s_mm, s_max, p_done, t_mm, t_act, t_dve = (sem(n) for n in ("s_mm", "s_max", "p_done", "t_mm", "t_act", "t_dve"))
    pv_mm, o_copy, o_mm, rl_done, o_div, o_add = (sem(n) for n in ("pv_mm", "o_copy", "o_mm", "rl_done", "o_div", "o_add"))
    o_out = [sem(f"o_out{i}") for i in range(2)]

    def run(eng, batch, tail, tail_stores=False):
        batch(0, 0)
        if tail_stores:
            wait(eng, tail_out, TAIL_STORED)
        with eng.Fori(0, (B - 2) // LOOP_BATCHES) as turn:
            for k in range(LOOP_BATCHES):
                batch(turn * LOOP_BATCHES + (1 + k), (1 + k) % 2)
        batch(B - 1, (B - 1) % 2)
        tail(B, B % 2)

    def copied(p, b):
        if p in ACT_PAIRS:
            return t_act, len(ACT_PAIRS) * b + ACT_PAIRS.index(p) + 1
        return t_dve, len(DVE_PAIRS) * b + DVE_PAIRS.index(p) + 1

    def pairs_before(n, mine):
        return [(p, COPY_BEFORE[p] // TILES) for p in mine if COPY_BEFORE[p] % TILES == n]

    def copy_pair(eng, p, b, par):
        wait(eng, t_mm, TILES * b + 2 * p + 2)
        if p in (ACT_PAIRS[0], DVE_PAIRS[0]):
            wait(eng, pv_mm, CREDIT + b - 1)
        it, h = divmod(2 * p, HEADS)
        dst = p_t[par][:, h:h + 2, :, it * 128:(it + 1) * 128]
        src = ps_t[p % 2][:, :, :].rearrange("p h (j i) -> p h j i", j=T)
        return dst, src

    block = ctx.enter_context(nc.Block())

    @block.sync
    def _(sp):
        def load(b, par):
            if not (isinstance(b, int) and b == 0):
                wait(sp, s_mm, CREDIT + TILES * (b - 1))
                load_qk(sp, qk_dram, keep, b, par)
            wait(sp, pv_mm, CREDIT + b - 1)
            sp.dma_start(v_sb[par][:, :, :].rearrange("p t d -> p (t d)"), batch_of(v_dram, b).rearrange("o p n -> p (o n)")).then_inc(v_in[par], 16)
            wait(sp, o_add, CREDIT + b - 1)
            sp.dma_start(x1[par][:, :], batch_of(x1_dram, b).rearrange("o p t d -> p (o t d)")).then_inc(x_in[par], 16)

        def batch(b, par):
            first, last = (isinstance(b, int) and b == n for n in (0, B - 1))
            if not last:
                load(b + 1, 1 - par)
            if not first:
                store(b - 1, 1 - par)

        def store(b, par):
            wait(sp, o_add, CREDIT + b + 1)
            sp.dma_start(batch_of(out, b).rearrange("o (p t) d -> p (o t d)", t=T), o_n[par][:, :]).then_inc(o_out[par], 16)

        for s in o_out:
            sp.sem_inc(s, CREDIT)
        wait(sp, tail_out, TAIL_STORED)
        load(0, 0)
        run(sp, batch, lambda b, par: store(b - 1, 1 - par))
        for s in o_out:
            sp.wait_ge(s, CREDIT + 16 * B // 2)

    def parity_count(b, par, each):
        if isinstance(b, int):
            return each * (b // 2 + 1)
        assert each % 2 == 0
        return b * (each // 2) + (each // 2) * (2 - par)

    @block.gpsimd
    def _(pool):
        def batch(b, par):
            if isinstance(b, int) and b == 0:
                return
            c, cp = b - 1, 1 - par
            wait(pool, o_div, CREDIT + c + 1)
            wait(pool, x_in[cp], parity_count(c, cp, 16))
            pool.tensor_tensor(o_n[cp][:, :], o_n[cp][:, :], x1[cp][:, :], ALU.add).then_inc(o_add, 1)

        pool.sem_inc(o_add, CREDIT)
        run(pool, batch, batch)

    @block.scalar
    def _(act):
        def batch(b, par, tiles=TILES):
            first = isinstance(b, int) and b == 0
            for n in range(TILES):
                for p, back in pairs_before(n, ACT_PAIRS):
                    if (first and back) or not (tiles or back):
                        continue
                    dst, src = copy_pair(act, p, b - back, (par + back) % 2)
                    act.activation(dst, src, ACT.Copy).then_inc(t_act, 1)
                if n == OCOPY_AT and not first:
                    wait(act, pv_mm, CREDIT + b)
                    wait(act, o_mm, CREDIT + b - 1)
                    act.activation(o_t[:, :], ps_o[:, :], ACT.Copy).then_inc(o_copy, 1)
                if tiles:
                    wait(act, s_max, TILES * b + n + 1)
                    if n == 0:
                        wait(act, o_div, CREDIT + b - 1)
                    act.activation(s_ring[:, n % RING, :], s_ring[:, n % RING, :], ACT.Exp,
                                   bias=low[:, n:n + 1], scale=-1.0, accum_out=lsum[par][:, n:n + 1]).then_inc(p_done, 1)

        act.sem_inc(o_copy, CREDIT)
        run(act, batch, lambda b, par: batch(b, par, 0), tail_stores=True)

    @block.vector
    def _(dve):
        dve.wait_ge(mask_done, T)

        def batch(b, par, tiles=TILES):
            first = isinstance(b, int) and b == 0
            for n in range(TILES):
                for p, back in pairs_before(n, DVE_PAIRS):
                    if (first and back) or not (tiles or back):
                        continue
                    dst, src = copy_pair(dve, p, b - back, (par + back) % 2)
                    dve.tensor_copy(dst, src).then_inc(t_dve, 1)
                if tiles:
                    wait(dve, s_mm, CREDIT + TILES * b + n + 1)
                    wait(dve, t_mm, TILES * b + n - RING + 1)
                    settle(dve, waits_met)
                    dve.tensor_tensor_reduce(s_ring[:, n % RING, :], ps_s[S_BANK[n]][:, :], mask[:, n // HEADS, :],
                                             -SCALE, 3.0e38, ALU.add, ALU.min, low[:, n:n + 1]).then_inc(s_max, 1)
                if n == FIN_AT and not first:
                    c, cp = b - 1, 1 - par
                    wait(dve, p_done, TILES * b)
                    dve.reciprocal(lsum[cp][:, :], lsum[cp][:, :]).then_inc(rl_done, 1)
                    wait(dve, rl_done, b)
                    wait(dve, o_mm, CREDIT + b)
                    wait(dve, o_out[cp], CREDIT + parity_count(c, cp, 16) - 16)
                    dve.tensor_tensor(o_n[cp][:, :].rearrange("p (a e) -> p a e", e=HD),
                                      ps_n[:, :].rearrange("p (a e) -> p a e", e=HD),
                                      lsum[cp][:, :].rearrange("p (a o) -> p a o", o=1).to_broadcast([128, TILES, HD]),
                                      ALU.mult).then_inc(o_div, 1)

        dve.sem_inc(o_div, CREDIT)
        run(dve, batch, lambda b, par: batch(b, par, 0), tail_stores=True)

    @block.tensor
    def _(pe):
        def transposes(n, b):
            p = n // 2
            wait(pe, p_done, TILES * b + n + 1)
            if n % 2 == 0:
                s, value = copied(p - 2, b) if p >= 2 else copied(p - 2 + PAIRS, b - 1)
                if not (isinstance(b, int) and b == 0 and p < 2):
                    wait(pe, s, value)
            for j in range(T):
                mm = pe.transpose(ps_t[p % 2][:, n % 2, j * 128:(j + 1) * 128],
                                  s_ring[:, n % RING, j * 128:(j + 1) * 128], ident[:, :])
            mm.then_inc(t_mm, 1)

        def batch(b, par, tiles=TILES):
            first = isinstance(b, int) and b == 0
            c, cp = b - 1, 1 - par
            for n in range(TILES):
                it, h = divmod(n, HEADS)
                if tiles:
                    if n == 0:
                        wait(pe, qk_in[par], parity_count(b, par, 128))
                    wait(pe, s_max, TILES * b + n - S_BACK[n] + 1)
                    pe.matmul(ps_s[S_BANK[n]][:, :], q_st[par][:, h, it * 128:(it + 1) * 128],
                              k_st[par][:, h, :], start=True, stop=True).then_inc(s_mm, 1)
                if n >= LAG and tiles:
                    transposes(n - LAG, b)
                if n < LAG and not first:
                    transposes(TILES + n - LAG, c)
                for k in range(*PV_RANGE[n]) if not first else ():
                    j, hh = divmod(k, HEADS)
                    if k == 0:
                        for p in (ACT_PAIRS[-1], DVE_PAIRS[-1]):
                            wait(pe, *copied(p, c))
                        wait(pe, v_in[cp], parity_count(c, cp, 16))
                        wait(pe, o_div, CREDIT + c)
                    cols = slice(HD * hh, HD * (hh + 1))
                    mm = pe.matmul(ps_o[cols, :], v_sb[cp][:, j, cols], p_t[cp][:, hh, j, :],
                                   start=(j == 0), stop=(j == T - 1), tile_position=(0, HD * hh))
                    if k == HEADS * T - 1:
                        mm.then_inc(pv_mm, 1)
                if n == OT_AT and not first:
                    wait(pe, o_copy, CREDIT + b)
                    for t in range(T):
                        mm = pe.transpose(ps_n[:, t * 128:(t + 1) * 128], o_t[:, t * 128:(t + 1) * 128], ident[:, :])
                    mm.then_inc(o_mm, 1)

        pe.sem_inc(s_mm, CREDIT)
        pe.sem_inc(pv_mm, CREDIT)
        pe.sem_inc(o_mm, CREDIT)
        run(pe, batch, lambda b, par: batch(b, par, 0))


def graph_block(nc, x, adj, alpha, w, d, fcw, fcb, wqkv, out):
    x1_dram = nc.dram_tensor("x1_dram", [B, 128, T, D], F32, kind="Internal").ap()
    qk_dram = nc.dram_tensor("qk_dram", [B, 128, 4, N], F32, kind="Internal").ap()
    v_dram = nc.dram_tensor("v_dram", [B, 128, N], F32, kind="Internal").ap()
    keep = {}
    with ExitStack() as outer:
        keep["ident"] = outer.enter_context(nc.sbuf_tensor("ident", [128, 128], F32))
        keep["pH"] = [outer.enter_context(nc.sbuf_tensor(f"pH{k}", [128, T, N], F32R)) for k in range(3)]
        keep["pL"] = [outer.enter_context(nc.sbuf_tensor(f"pL{k}", [128, T, N], F32R)) for k in range(3)]
        assert HEADS == T
        keep["q_st"], keep["k_st"] = keep["pH"][0::2], keep["pL"][0::2]
        for name in ("adj_in", "mask_done", "tail_out"):
            keep[name] = outer.enter_context(nc.semaphore("att_" + name))
        keep["qk_in"] = [outer.enter_context(nc.semaphore(f"qk_in{i}")) for i in range(2)]
        with ExitStack() as kept:
            def sb(name, shape, dt=F32R):
                return kept.enter_context(nc.sbuf_tensor(name, shape, dt))
            keep["rH"], keep["rL"] = sb("rH", [128, 3, 3 * D]), sb("rL", [128, 3, 3 * D])
            keep["wH"], keep["wL"] = sb("wH", [128, 3 * D]), sb("wL", [128, 3 * D])
            keep["g"] = sb("g", [128, T, 3 * D], F32)
            ln = FirstNorm(sb, lambda name: kept.enter_context(nc.semaphore(name)))
            with ExitStack() as ctx:
                setup_block(nc, ctx, x, adj, alpha, w, d, fcw, fcb, wqkv, keep, ln)
            with ExitStack() as ctx:
                ode_block(nc, ctx, x, adj, x1_dram, qk_dram, v_dram, keep, ln)
        with ExitStack() as ctx:
            attention_block(nc, ctx, x1_dram, qk_dram, v_dram, out, keep)


_INS = ["x", "adj", "L0_gnn_alpha_train", "L0_gnn_w", "L0_gnn_d", "L0_gnn_fc_in_w", "L0_gnn_fc_in_b", "L1_gnn_W"]


def kernel(**inputs):
    import numpy as np
    import concourse.bacc as bacc
    from concourse.bass_utils import run_bass_kernel_spmd

    nc = bacc.Bacc("TRN2", target_bir_lowering=False, num_devices=1)
    arrays, args = {}, []
    for name in _INS:
        a = np.ascontiguousarray(inputs[name])
        arrays[f"in_{name}"] = a
        args.append(nc.dram_tensor(f"in_{name}", a.shape, mybir.dt.from_np(a.dtype), kind="ExternalInput").ap())
    args.append(nc.dram_tensor("out_x", (B, N, D), F32, kind="ExternalOutput").ap())
    graph_block(nc, *args)
    r = run_bass_kernel_spmd(nc, [arrays], core_ids=[0])
    return r.results[0]["out_x"]
```
